# Optimizing a Trainium2 kernel written in Bass

```python
import numpy as np
import jax
import jax.numpy as jnp

def _softmax(x, axis=-1):
    return jax.nn.softmax(x, axis=axis)

def _gelu(x):
    return jax.nn.gelu(x, approximate=True)

def _silu(x):
    return jax.nn.silu(x)

def _sigmoid(x):
    return jax.nn.sigmoid(x)

def _layernorm(x, axis=-1, eps=1e-05):
    m = jnp.mean(x, axis=axis, keepdims=True)
    v = jnp.var(x, axis=axis, keepdims=True)
    return (x - m) / jnp.sqrt(v + eps)

def _scatter_add(tgt, idx, src, axis=0):
    return tgt.at[idx].add(src)

def _segment_sum(src, seg, n):
    return jax.ops.segment_sum(src, seg, n)
kernel_name = 'mk_xattn_seq_d4_seqx_r4_45b73f'

def setup_inputs(seed: int=0):
    np.random.seed(seed)
    _w = jnp.asarray

    def _rec_inputs():
        import jax
        import jax.numpy as jnp
        _rk = jax.random.key(seed)
        x = -0.0002928 + 1 * jax.random.normal(jax.random.fold_in(_rk, 1), (8, 512, 256), jnp.float32)
        _lenS = 512 - jax.random.randint(jax.random.fold_in(_rk, 7), (8,), 0, max(1, 512 // 4) + 1, jnp.int32)
        _lenS2 = 512 - jax.random.randint(jax.random.fold_in(_rk, 8), (8,), 0, max(1, 512 // 4) + 1, jnp.int32)
        _ctx_1024P = jax.random.normal(jax.random.fold_in(_rk, 11), (8, 16, 256), jnp.float32)
        _ctx_1024c = jax.random.dirichlet(jax.random.fold_in(_rk, 511), 0.3 * jnp.ones((16,), jnp.float32), (8, 512))
        _ctx_1024t = jnp.einsum('bsk,bkd->bsd', _ctx_1024c, _ctx_1024P)
        _ctx_1024t = _ctx_1024t * jax.lax.rsqrt(jnp.mean(jnp.square(_ctx_1024t)) + 1e-12) * 0.953939
        ctx_1024 = -1.39393e-06 + 0.999914 * (_ctx_1024t + 0.3 * jax.random.normal(jax.random.fold_in(_rk, 611), (8, 512, 256), jnp.float32))
        _validS = jnp.arange(512)[None, :] < _lenS[:, None]
        _validS2 = jnp.arange(512)[None, :] < _lenS2[:, None]
        _causal = jnp.tril(jnp.ones((512, 512), dtype=bool))
        mask_BxSxS2_bk0 = jnp.logical_not(jnp.broadcast_to(_validS2[:, None, :], (8, 512, 512)))
        mask_SxS_bk1 = jnp.broadcast_to(_validS[0:1, :], (512, 512))
        return (x, ctx_1024, mask_BxSxS2_bk0, mask_SxS_bk1)
    x, ctx_1024, mask_BxSxS2_bk0, mask_SxS_bk1 = _rec_inputs()

    def _L0_xattn_setup():
        import jax, jax.numpy as jnp
        import numpy as np
        EPS = 1e-05

        def layer_norm(x, w, b):
            mu = jnp.mean(x, axis=-1, keepdims=True)
            var = jnp.var(x, axis=-1, keepdims=True)
            return (x - mu) * jax.lax.rsqrt(var + EPS) * w + b
        key = jax.random.key(seed)
        ks = jax.random.split(key, 12)
        B, N, M, C = (2, 512, 512, 256)
        H = 16
        hid = 4 * C
        s = lambda d: 1.0 / np.sqrt(d)
        return {'x': jax.random.normal(ks[0], (B, N, C), jnp.float32), 'context': jax.random.normal(ks[1], (B, M, C), jnp.float32), 'xa_mask': jax.random.bernoulli(ks[2], 0.1, (B, N, M)), 'qn_w': jnp.ones((C,), jnp.float32), 'qn_b': jnp.zeros((C,), jnp.float32), 'cn_w': jnp.ones((C,), jnp.float32), 'cn_b': jnp.zeros((C,), jnp.float32), 'n2_w': jnp.ones((C,), jnp.float32), 'n2_b': jnp.zeros((C,), jnp.float32), 'q_w': jax.random.normal(ks[3], (C, C), jnp.float32) * s(C), 'kv_w': jax.random.normal(ks[4], (C, 2 * C), jnp.float32) * s(C), 'proj_w': jax.random.normal(ks[5], (C, C), jnp.float32) * s(C), 'proj_b': jnp.zeros((C,), jnp.float32), 'fc1_w': jax.random.normal(ks[6], (C, hid), jnp.float32) * s(C), 'fc1_b': jnp.zeros((hid,), jnp.float32), 'fc2_w': jax.random.normal(ks[7], (hid, C), jnp.float32) * s(hid), 'fc2_b': jnp.zeros((C,), jnp.float32)}
    _L0_xattn_all = _L0_xattn_setup()
    _L0_xattn_in = {k: v for k, v in _L0_xattn_all.items() if k in ('qn_w', 'qn_b', 'cn_w', 'cn_b', 'n2_w', 'n2_b', 'q_w', 'kv_w', 'proj_w', 'proj_b', 'fc1_w', 'fc1_b', 'fc2_w', 'fc2_b')}
    del _L0_xattn_all

    def _L1_xattn_setup():
        import jax, jax.numpy as jnp
        import numpy as np
        B, S, D, H, FF = (2, 512, 256, 16, 1024)
        DH = D // H
        EPS = 1e-05

        def _layernorm(x, g, b):
            mu = jnp.mean(x, axis=-1, keepdims=True)
            var = jnp.var(x, axis=-1, keepdims=True)
            return (x - mu) * jax.lax.rsqrt(var + EPS) * g + b

        def _attn(xq, xkv, qw, qb, kw, kb, vw, vb, ow, ob, mask):
            Bq, Sq, Dm = xq.shape
            Sk = xkv.shape[1]
            scale = jnp.asarray(DH, xq.dtype) ** (-0.5)
            q = (xq @ qw + qb).reshape(Bq, Sq, H, DH).transpose(0, 2, 1, 3)
            k = (xkv @ kw + kb).reshape(Bq, Sk, H, DH).transpose(0, 2, 1, 3)
            v = (xkv @ vw + vb).reshape(Bq, Sk, H, DH).transpose(0, 2, 1, 3)
            scores = jnp.einsum('bhqd,bhkd->bhqk', q, k) * scale
            if mask is not None:
                scores = jnp.where(mask[None, None], -jnp.inf, scores)
            attn = jax.nn.softmax(scores, axis=-1)
            out = jnp.einsum('bhqk,bhkd->bhqd', attn, v).transpose(0, 2, 1, 3).reshape(Bq, Sq, Dm)
            return out @ ow + ob
        key = jax.random.key(seed)
        ks = jax.random.split(key, 32)
        s = 0.02

        def lin(i, din, dout):
            return (jax.random.normal(ks[i], (din, dout), jnp.float32) * s, jnp.zeros((dout,), jnp.float32))
        inp = {}
        inp['queries'] = jax.random.normal(ks[0], (B, S, D), jnp.float32)
        inp['memory'] = jax.random.normal(ks[1], (B, S, D), jnp.float32)
        inp['causal_mask'] = jnp.triu(jnp.ones((S, S), jnp.bool_), k=1)
        inp['ca_qw'], inp['ca_qb'] = lin(2, D, D)
        inp['ca_kw'], inp['ca_kb'] = lin(3, D, D)
        inp['ca_vw'], inp['ca_vb'] = lin(4, D, D)
        inp['ca_ow'], inp['ca_ob'] = lin(5, D, D)
        inp['sa_qw'], inp['sa_qb'] = lin(6, D, D)
        inp['sa_kw'], inp['sa_kb'] = lin(7, D, D)
        inp['sa_vw'], inp['sa_vb'] = lin(8, D, D)
        inp['sa_ow'], inp['sa_ob'] = lin(9, D, D)
        inp['w1'], inp['b1'] = lin(10, D, FF)
        inp['w2'], inp['b2'] = lin(11, FF, D)
        for i, nm in enumerate(['ln1', 'ln2', 'ln3']):
            inp[nm + '_g'] = jnp.ones((D,), jnp.float32)
            inp[nm + '_b'] = jnp.zeros((D,), jnp.float32)
        return inp
    _L1_xattn_all = _L1_xattn_setup()
    _L1_xattn_in = {k: v for k, v in _L1_xattn_all.items() if k in ('ca_qw', 'ca_qb', 'ca_kw', 'ca_kb', 'ca_vw', 'ca_vb', 'ca_ow', 'ca_ob', 'sa_qw', 'sa_qb', 'sa_kw', 'sa_kb', 'sa_vw', 'sa_vb', 'sa_ow', 'sa_ob', 'w1', 'b1', 'w2', 'b2', 'ln1_g', 'ln1_b', 'ln2_g', 'ln2_b', 'ln3_g', 'ln3_b')}
    del _L1_xattn_all

    def _L2_xattn_setup():
        import jax, jax.numpy as jnp
        import numpy as np
        DIM = 256
        HEADS = 16
        HEAD_DIM = DIM // HEADS
        HIDDEN = int(DIM * 4.0)
        SCALE = HEAD_DIM ** (-0.5)
        EPS = 1e-05

        def _ln(x, g, b):
            m = jnp.mean(x, axis=-1, keepdims=True)
            v = jnp.mean((x - m) ** 2, axis=-1, keepdims=True)
            return (x - m) * jax.lax.rsqrt(v + EPS) * g + b

        def _split_heads(t, B, N):
            return t.reshape(B, N, HEADS, HEAD_DIM).transpose(0, 2, 1, 3)
        key = jax.random.key(seed)
        ks = jax.random.split(key, 16)
        B, Nt, Ni = (4, 256, 144)
        s = lambda fan_in: 1.0 / np.sqrt(fan_in)
        return {'x': jax.random.normal(ks[0], (B, Nt, DIM), jnp.float32), 'encoder_hidden_state': jax.random.normal(ks[1], (B, Ni, DIM), jnp.float32), 'ln1_g': jnp.ones((DIM,), jnp.float32), 'ln1_b': jnp.zeros((DIM,), jnp.float32), 'w_qkv': jax.random.uniform(ks[2], (3 * DIM, DIM), jnp.float32, -s(DIM), s(DIM)), 'w_prj1': jax.random.uniform(ks[3], (DIM, DIM), jnp.float32, -s(DIM), s(DIM)), 'b_prj1': jnp.zeros((DIM,), jnp.float32), 'ln2_g': jnp.ones((DIM,), jnp.float32), 'ln2_b': jnp.zeros((DIM,), jnp.float32), 'w_q': jax.random.uniform(ks[4], (DIM, DIM), jnp.float32, -s(DIM), s(DIM)), 'w_kv': jax.random.uniform(ks[5], (2 * DIM, DIM), jnp.float32, -s(DIM), s(DIM)), 'w_prj2': jax.random.uniform(ks[6], (DIM, DIM), jnp.float32, -s(DIM), s(DIM)), 'b_prj2': jnp.zeros((DIM,), jnp.float32), 'ln3_g': jnp.ones((DIM,), jnp.float32), 'ln3_b': jnp.zeros((DIM,), jnp.float32), 'w_fc1': jax.random.uniform(ks[7], (HIDDEN, DIM), jnp.float32, -s(DIM), s(DIM)), 'b_fc1': jnp.zeros((HIDDEN,), jnp.float32), 'w_fc2': jax.random.uniform(ks[8], (DIM, HIDDEN), jnp.float32, -s(HIDDEN), s(HIDDEN)), 'b_fc2': jnp.zeros((DIM,), jnp.float32)}
    _L2_xattn_all = _L2_xattn_setup()
    _L2_xattn_in = {k: v for k, v in _L2_xattn_all.items() if k in ('ln1_g', 'ln1_b', 'w_qkv', 'w_prj1', 'b_prj1', 'ln2_g', 'ln2_b', 'w_q', 'w_kv', 'w_prj2', 'b_prj2', 'ln3_g', 'ln3_b', 'w_fc1', 'b_fc1', 'w_fc2', 'b_fc2')}
    del _L2_xattn_all

    def _L3_xattn_setup():
        import jax, jax.numpy as jnp
        import numpy as np
        B, Q, KV = (2, 512, 512)
        D_MODEL = 256
        N_HEADS = 16
        D_KV = 64
        EPS = 1e-06
        key = jax.random.key(seed)
        ks = jax.random.split(key, 7)
        s = 0.02
        return {'hidden_states': jax.random.normal(ks[0], (B, Q, D_MODEL), jnp.float32), 'key_value_states': jax.random.normal(ks[1], (B, KV, D_MODEL), jnp.float32), 'wq': jax.random.normal(ks[2], (D_MODEL, N_HEADS * D_KV), jnp.float32) * s, 'wk': jax.random.normal(ks[3], (D_MODEL, N_HEADS * D_KV), jnp.float32) * s, 'wv': jax.random.normal(ks[4], (D_MODEL, N_HEADS * D_KV), jnp.float32) * s, 'wo': jax.random.normal(ks[5], (N_HEADS * D_KV, D_MODEL), jnp.float32) * s, 'norm_w': jnp.ones((D_MODEL,), jnp.float32)}
    _L3_xattn_all = _L3_xattn_setup()
    _L3_xattn_in = {k: v for k, v in _L3_xattn_all.items() if k in ('wq', 'wk', 'wv', 'wo', 'norm_w')}
    del _L3_xattn_all
    return {'x': x, 'ctx_1024': ctx_1024, 'mask_BxSxS2_bk0': mask_BxSxS2_bk0, 'mask_SxS_bk1': mask_SxS_bk1, 'L0_xattn_qn_w': _L0_xattn_in['qn_w'], 'L0_xattn_qn_b': _L0_xattn_in['qn_b'], 'L0_xattn_cn_w': _L0_xattn_in['cn_w'], 'L0_xattn_cn_b': _L0_xattn_in['cn_b'], 'L0_xattn_n2_w': _L0_xattn_in['n2_w'], 'L0_xattn_n2_b': _L0_xattn_in['n2_b'], 'L0_xattn_q_w': _L0_xattn_in['q_w'], 'L0_xattn_kv_w': _L0_xattn_in['kv_w'], 'L0_xattn_proj_w': _L0_xattn_in['proj_w'], 'L0_xattn_proj_b': _L0_xattn_in['proj_b'], 'L0_xattn_fc1_w': _L0_xattn_in['fc1_w'], 'L0_xattn_fc1_b': _L0_xattn_in['fc1_b'], 'L0_xattn_fc2_w': _L0_xattn_in['fc2_w'], 'L0_xattn_fc2_b': _L0_xattn_in['fc2_b'], 'L1_xattn_ca_qw': _L1_xattn_in['ca_qw'], 'L1_xattn_ca_qb': _L1_xattn_in['ca_qb'], 'L1_xattn_ca_kw': _L1_xattn_in['ca_kw'], 'L1_xattn_ca_kb': _L1_xattn_in['ca_kb'], 'L1_xattn_ca_vw': _L1_xattn_in['ca_vw'], 'L1_xattn_ca_vb': _L1_xattn_in['ca_vb'], 'L1_xattn_ca_ow': _L1_xattn_in['ca_ow'], 'L1_xattn_ca_ob': _L1_xattn_in['ca_ob'], 'L1_xattn_sa_qw': _L1_xattn_in['sa_qw'], 'L1_xattn_sa_qb': _L1_xattn_in['sa_qb'], 'L1_xattn_sa_kw': _L1_xattn_in['sa_kw'], 'L1_xattn_sa_kb': _L1_xattn_in['sa_kb'], 'L1_xattn_sa_vw': _L1_xattn_in['sa_vw'], 'L1_xattn_sa_vb': _L1_xattn_in['sa_vb'], 'L1_xattn_sa_ow': _L1_xattn_in['sa_ow'], 'L1_xattn_sa_ob': _L1_xattn_in['sa_ob'], 'L1_xattn_w1': _L1_xattn_in['w1'], 'L1_xattn_b1': _L1_xattn_in['b1'], 'L1_xattn_w2': _L1_xattn_in['w2'], 'L1_xattn_b2': _L1_xattn_in['b2'], 'L1_xattn_ln1_g': _L1_xattn_in['ln1_g'], 'L1_xattn_ln1_b': _L1_xattn_in['ln1_b'], 'L1_xattn_ln2_g': _L1_xattn_in['ln2_g'], 'L1_xattn_ln2_b': _L1_xattn_in['ln2_b'], 'L1_xattn_ln3_g': _L1_xattn_in['ln3_g'], 'L1_xattn_ln3_b': _L1_xattn_in['ln3_b'], 'L2_xattn_ln1_g': _L2_xattn_in['ln1_g'], 'L2_xattn_ln1_b': _L2_xattn_in['ln1_b'], 'L2_xattn_w_qkv': _L2_xattn_in['w_qkv'], 'L2_xattn_w_prj1': _L2_xattn_in['w_prj1'], 'L2_xattn_b_prj1': _L2_xattn_in['b_prj1'], 'L2_xattn_ln2_g': _L2_xattn_in['ln2_g'], 'L2_xattn_ln2_b': _L2_xattn_in['ln2_b'], 'L2_xattn_w_q': _L2_xattn_in['w_q'], 'L2_xattn_w_kv': _L2_xattn_in['w_kv'], 'L2_xattn_w_prj2': _L2_xattn_in['w_prj2'], 'L2_xattn_b_prj2': _L2_xattn_in['b_prj2'], 'L2_xattn_ln3_g': _L2_xattn_in['ln3_g'], 'L2_xattn_ln3_b': _L2_xattn_in['ln3_b'], 'L2_xattn_w_fc1': _L2_xattn_in['w_fc1'], 'L2_xattn_b_fc1': _L2_xattn_in['b_fc1'], 'L2_xattn_w_fc2': _L2_xattn_in['w_fc2'], 'L2_xattn_b_fc2': _L2_xattn_in['b_fc2'], 'L3_xattn_wq': _L3_xattn_in['wq'], 'L3_xattn_wk': _L3_xattn_in['wk'], 'L3_xattn_wv': _L3_xattn_in['wv'], 'L3_xattn_wo': _L3_xattn_in['wo'], 'L3_xattn_norm_w': _L3_xattn_in['norm_w']}

def reference(x, ctx_1024, mask_BxSxS2_bk0, mask_SxS_bk1, L0_xattn_qn_w, L0_xattn_qn_b, L0_xattn_cn_w, L0_xattn_cn_b, L0_xattn_n2_w, L0_xattn_n2_b, L0_xattn_q_w, L0_xattn_kv_w, L0_xattn_proj_w, L0_xattn_proj_b, L0_xattn_fc1_w, L0_xattn_fc1_b, L0_xattn_fc2_w, L0_xattn_fc2_b, L1_xattn_ca_qw, L1_xattn_ca_qb, L1_xattn_ca_kw, L1_xattn_ca_kb, L1_xattn_ca_vw, L1_xattn_ca_vb, L1_xattn_ca_ow, L1_xattn_ca_ob, L1_xattn_sa_qw, L1_xattn_sa_qb, L1_xattn_sa_kw, L1_xattn_sa_kb, L1_xattn_sa_vw, L1_xattn_sa_vb, L1_xattn_sa_ow, L1_xattn_sa_ob, L1_xattn_w1, L1_xattn_b1, L1_xattn_w2, L1_xattn_b2, L1_xattn_ln1_g, L1_xattn_ln1_b, L1_xattn_ln2_g, L1_xattn_ln2_b, L1_xattn_ln3_g, L1_xattn_ln3_b, L2_xattn_ln1_g, L2_xattn_ln1_b, L2_xattn_w_qkv, L2_xattn_w_prj1, L2_xattn_b_prj1, L2_xattn_ln2_g, L2_xattn_ln2_b, L2_xattn_w_q, L2_xattn_w_kv, L2_xattn_w_prj2, L2_xattn_b_prj2, L2_xattn_ln3_g, L2_xattn_ln3_b, L2_xattn_w_fc1, L2_xattn_b_fc1, L2_xattn_w_fc2, L2_xattn_b_fc2, L3_xattn_wq, L3_xattn_wk, L3_xattn_wv, L3_xattn_wo, L3_xattn_norm_w):
    import jax
    import jax.numpy as jnp

    def _L0_xattn_ref(x, context, xa_mask, qn_w, qn_b, cn_w, cn_b, n2_w, n2_b, q_w, kv_w, proj_w, proj_b, fc1_w, fc1_b, fc2_w, fc2_b):
        import jax, jax.numpy as jnp
        import numpy as np
        EPS = 1e-05

        def layer_norm(x, w, b):
            mu = jnp.mean(x, axis=-1, keepdims=True)
            var = jnp.var(x, axis=-1, keepdims=True)
            return (x - mu) * jax.lax.rsqrt(var + EPS) * w + b
        B, N, C = x.shape
        M = context.shape[1]
        H = 16
        D = C // H
        scale = D ** (-0.5)
        xq = layer_norm(x, qn_w, qn_b)
        ctx = layer_norm(context, cn_w, cn_b)
        q = (xq @ q_w).reshape(B, N, H, D)
        kv = (ctx @ kv_w).reshape(B, M, 2, H, D)
        k, v = (kv[:, :, 0], kv[:, :, 1])
        attn = jnp.einsum('bnhd,bmhd->bhnm', q, k) * scale
        neg = -jnp.finfo(attn.dtype).max
        attn = jnp.where(xa_mask[:, None, :, :], neg, attn)
        attn = jax.nn.softmax(attn, axis=-1)
        out = jnp.einsum('bhnm,bmhd->bnhd', attn, v).reshape(B, N, C)
        out = out @ proj_w + proj_b
        x = x + out
        h = layer_norm(x, n2_w, n2_b)
        h = jax.nn.gelu(h @ fc1_w + fc1_b, approximate=False) @ fc2_w + fc2_b
        return x + h

    def _L1_xattn_ref(queries, memory, causal_mask, ca_qw, ca_qb, ca_kw, ca_kb, ca_vw, ca_vb, ca_ow, ca_ob, sa_qw, sa_qb, sa_kw, sa_kb, sa_vw, sa_vb, sa_ow, sa_ob, w1, b1, w2, b2, ln1_g, ln1_b, ln2_g, ln2_b, ln3_g, ln3_b):
        import jax, jax.numpy as jnp
        import numpy as np
        B, S, D, H, FF = (2, 512, 256, 16, 1024)
        DH = D // H
        EPS = 1e-05

        def _layernorm(x, g, b):
            mu = jnp.mean(x, axis=-1, keepdims=True)
            var = jnp.var(x, axis=-1, keepdims=True)
            return (x - mu) * jax.lax.rsqrt(var + EPS) * g + b

        def _attn(xq, xkv, qw, qb, kw, kb, vw, vb, ow, ob, mask):
            Bq, Sq, Dm = xq.shape
            Sk = xkv.shape[1]
            scale = jnp.asarray(DH, xq.dtype) ** (-0.5)
            q = (xq @ qw + qb).reshape(Bq, Sq, H, DH).transpose(0, 2, 1, 3)
            k = (xkv @ kw + kb).reshape(Bq, Sk, H, DH).transpose(0, 2, 1, 3)
            v = (xkv @ vw + vb).reshape(Bq, Sk, H, DH).transpose(0, 2, 1, 3)
            scores = jnp.einsum('bhqd,bhkd->bhqk', q, k) * scale
            if mask is not None:
                scores = jnp.where(mask[None, None], -jnp.inf, scores)
            attn = jax.nn.softmax(scores, axis=-1)
            out = jnp.einsum('bhqk,bhkd->bhqd', attn, v).transpose(0, 2, 1, 3).reshape(Bq, Sq, Dm)
            return out @ ow + ob
        q = _layernorm(queries, ln1_g, ln1_b)
        h = _attn(q, memory, ca_qw, ca_qb, ca_kw, ca_kb, ca_vw, ca_vb, ca_ow, ca_ob, None)
        x = queries + h
        q = _layernorm(x, ln2_g, ln2_b)
        h = _attn(q, q, sa_qw, sa_qb, sa_kw, sa_kb, sa_vw, sa_vb, sa_ow, sa_ob, causal_mask)
        x = x + h
        q = _layernorm(x, ln3_g, ln3_b)
        x = x + (jax.nn.gelu(q @ w1 + b1, approximate=False) @ w2 + b2)
        return x

    def _L2_xattn_ref(x, encoder_hidden_state, ln1_g, ln1_b, w_qkv, w_prj1, b_prj1, ln2_g, ln2_b, w_q, w_kv, w_prj2, b_prj2, ln3_g, ln3_b, w_fc1, b_fc1, w_fc2, b_fc2):
        import jax, jax.numpy as jnp
        import numpy as np
        DIM = 256
        HEADS = 16
        HEAD_DIM = DIM // HEADS
        HIDDEN = int(DIM * 4.0)
        SCALE = HEAD_DIM ** (-0.5)
        EPS = 1e-05

        def _ln(x, g, b):
            m = jnp.mean(x, axis=-1, keepdims=True)
            v = jnp.mean((x - m) ** 2, axis=-1, keepdims=True)
            return (x - m) * jax.lax.rsqrt(v + EPS) * g + b

        def _split_heads(t, B, N):
            return t.reshape(B, N, HEADS, HEAD_DIM).transpose(0, 2, 1, 3)
        B, Nt, C = x.shape
        Ni = encoder_hidden_state.shape[1]
        h = _ln(x, ln1_g, ln1_b)
        qkv = h @ w_qkv.T
        q, k, v = jnp.split(qkv, 3, axis=-1)
        q, k, v = (_split_heads(q, B, Nt), _split_heads(k, B, Nt), _split_heads(v, B, Nt))
        attn = jnp.einsum('bhqd,bhkd->bhqk', q, k) * SCALE
        causal = jnp.tril(jnp.ones((Nt, Nt), bool))
        attn = jnp.where(causal, attn, -jnp.inf)
        attn = jax.nn.softmax(attn, axis=-1)
        o = jnp.einsum('bhqk,bhkd->bhqd', attn, v).transpose(0, 2, 1, 3).reshape(B, Nt, C)
        x = x + o @ w_prj1.T + b_prj1
        h = _ln(x, ln2_g, ln2_b)
        q = _split_heads(h @ w_q.T, B, Nt)
        kv = encoder_hidden_state @ w_kv.T
        k, v = jnp.split(kv, 2, axis=-1)
        k, v = (_split_heads(k, B, Ni), _split_heads(v, B, Ni))
        attn = jnp.einsum('bhqd,bhkd->bhqk', q, k) * SCALE
        attn = jax.nn.softmax(attn, axis=-1)
        o = jnp.einsum('bhqk,bhkd->bhqd', attn, v).transpose(0, 2, 1, 3).reshape(B, Nt, C)
        x = x + o @ w_prj2.T + b_prj2
        h = _ln(x, ln3_g, ln3_b)
        h = jax.nn.gelu(h @ w_fc1.T + b_fc1, approximate=False)
        x = x + h @ w_fc2.T + b_fc2
        return x

    def _L3_xattn_ref(hidden_states, key_value_states, wq, wk, wv, wo, norm_w):
        import jax, jax.numpy as jnp
        import numpy as np
        B, Q, KV = (2, 512, 512)
        D_MODEL = 256
        N_HEADS = 16
        D_KV = 64
        EPS = 1e-06
        var = jnp.mean(jnp.square(hidden_states), axis=-1, keepdims=True)
        normed = hidden_states * jax.lax.rsqrt(var + EPS) * norm_w
        b, q_len, _ = hidden_states.shape
        kv_len = key_value_states.shape[1]

        def split_heads(x):
            return x.reshape(b, -1, N_HEADS, D_KV).transpose(0, 2, 1, 3)
        q = split_heads(normed @ wq)
        k = split_heads(key_value_states @ wk)
        v = split_heads(key_value_states @ wv)
        scores = jnp.einsum('bhqd,bhkd->bhqk', q, k)
        attn = jax.nn.softmax(scores.astype(jnp.float32), axis=-1).astype(scores.dtype)
        ctx = jnp.einsum('bhqk,bhkd->bhqd', attn, v)
        ctx = ctx.transpose(0, 2, 1, 3).reshape(b, q_len, N_HEADS * D_KV)
        attn_out = ctx @ wo
        return hidden_states + attn_out
    x = _L0_xattn_ref(x, ctx_1024, mask_BxSxS2_bk0, L0_xattn_qn_w, L0_xattn_qn_b, L0_xattn_cn_w, L0_xattn_cn_b, L0_xattn_n2_w, L0_xattn_n2_b, L0_xattn_q_w, L0_xattn_kv_w, L0_xattn_proj_w, L0_xattn_proj_b, L0_xattn_fc1_w, L0_xattn_fc1_b, L0_xattn_fc2_w, L0_xattn_fc2_b)
    x = _L1_xattn_ref(x, ctx_1024, mask_SxS_bk1, L1_xattn_ca_qw, L1_xattn_ca_qb, L1_xattn_ca_kw, L1_xattn_ca_kb, L1_xattn_ca_vw, L1_xattn_ca_vb, L1_xattn_ca_ow, L1_xattn_ca_ob, L1_xattn_sa_qw, L1_xattn_sa_qb, L1_xattn_sa_kw, L1_xattn_sa_kb, L1_xattn_sa_vw, L1_xattn_sa_vb, L1_xattn_sa_ow, L1_xattn_sa_ob, L1_xattn_w1, L1_xattn_b1, L1_xattn_w2, L1_xattn_b2, L1_xattn_ln1_g, L1_xattn_ln1_b, L1_xattn_ln2_g, L1_xattn_ln2_b, L1_xattn_ln3_g, L1_xattn_ln3_b)
    x = _L2_xattn_ref(x, ctx_1024, L2_xattn_ln1_g, L2_xattn_ln1_b, L2_xattn_w_qkv, L2_xattn_w_prj1, L2_xattn_b_prj1, L2_xattn_ln2_g, L2_xattn_ln2_b, L2_xattn_w_q, L2_xattn_w_kv, L2_xattn_w_prj2, L2_xattn_b_prj2, L2_xattn_ln3_g, L2_xattn_ln3_b, L2_xattn_w_fc1, L2_xattn_b_fc1, L2_xattn_w_fc2, L2_xattn_b_fc2)
    x = _L3_xattn_ref(x, ctx_1024, L3_xattn_wq, L3_xattn_wk, L3_xattn_wv, L3_xattn_wo, L3_xattn_norm_w)
    return x

_drawn_inputs = setup_inputs


def setup_inputs(seed=0):
    import zlib

    import numpy as np

    out = dict(_drawn_inputs(seed))
    spreads = {'L0_xattn_qn_w': (1.0, 0.2),
     'L0_xattn_qn_b': (0.0, 0.414),
     'L0_xattn_cn_w': (1.0, 0.2),
     'L0_xattn_cn_b': (0.0, 0.1),
     'L0_xattn_n2_w': (1.0, 0.2),
     'L0_xattn_n2_b': (0.0, 0.1),
     'L0_xattn_proj_b': (0.0, 0.1),
     'L0_xattn_fc1_b': (0.0, 0.1),
     'L0_xattn_fc2_b': (0.0, 0.1),
     'L1_xattn_ca_qb': (0.0, 0.8),
     'L1_xattn_ca_kb': (0.0, 0.8),
     'L1_xattn_ca_vb': (0.0, 0.332),
     'L1_xattn_ca_ob': (0.0, 0.1),
     'L1_xattn_sa_qb': (0.0, 0.8),
     'L1_xattn_sa_kb': (0.0, 0.8),
     'L1_xattn_sa_vb': (0.0, 0.304),
     'L1_xattn_sa_ob': (0.0, 0.1),
     'L1_xattn_b1': (0.0, 0.301),
     'L1_xattn_b2': (0.0, 0.1),
     'L1_xattn_ln1_g': (1.0, 0.6),
     'L1_xattn_ln1_b': (0.0, 0.8),
     'L1_xattn_ln2_g': (1.0, 0.6),
     'L1_xattn_ln2_b': (0.0, 0.8),
     'L1_xattn_ln3_g': (1.0, 0.6),
     'L1_xattn_ln3_b': (0.0, 0.8),
     'L2_xattn_ln1_g': (1.0, 0.6),
     'L2_xattn_ln1_b': (0.0, 0.323),
     'L2_xattn_b_prj1': (0.0, 0.1),
     'L2_xattn_ln2_g': (1.0, 0.6),
     'L2_xattn_ln2_b': (0.0, 0.8),
     'L2_xattn_b_prj2': (0.0, 0.1),
     'L2_xattn_ln3_g': (1.0, 0.2),
     'L2_xattn_ln3_b': (0.0, 0.522),
     'L2_xattn_b_fc1': (0.0, 0.3),
     'L2_xattn_b_fc2': (0.0, 0.1),
     'L3_xattn_norm_w': (1.0, 0.6)}
    factors = {'L1_xattn_ca_qw': 8.0,
     'L1_xattn_ca_kw': 8.0,
     'L1_xattn_sa_qw': 8.0,
     'L1_xattn_sa_kw': 8.0,
     'L2_xattn_w_q': 3.725}
    for name, (base, spread) in spreads.items():
        noise = np.random.default_rng([zlib.crc32(name.encode()), seed]).standard_normal(out[name].shape)
        drawn = base * np.exp(spread * noise) if base else spread * noise
        out[name] = jnp.asarray(drawn.astype(out[name].dtype))
    for name, factor in factors.items():
        out[name] = (out[name] * factor).astype(out[name].dtype)
    return out
```

```python
from contextlib import ExitStack

import numpy as np
import concourse.bass as bass
from concourse import mybir

P = 128
B = 8
S = 512
D = 256
C = D // P
T = S // P
H = 16
DH = D // H
DL = 64
HL = H * DL
FF = 4 * D
FC = FF // P
G = H // 4
GB = P // DH
NP = H // 2
ROWS = 6 * DH
KROWS = ROWS + 3
BIG = 2.0 ** 100
LEAD = 6
LN_EPS, RMS_EPS = 1e-5, 1e-6

F32 = mybir.dt.float32
BF16 = mybir.dt.bfloat16
U8 = mybir.dt.uint8
ALU = mybir.AluOpType
ACT = mybir.ActivationFunctionType
AX = mybir.AxisListType.X

STAGES = range(6)
OWN_KEYS = (2, 3)
MASKED = (0, 2)
CAUSAL = 3
BIASED = (1, 2)
MLP = (0, 2, 4)
NORMS = (3, 1, 2, 1, 2, 1)

Q_SLOTS = (0, 0, 0, 1, 1, 2)
K_SLOTS = (0, 1, 2, 0, 1, 0)


def small_uses(s):
    uses = ["x0", "x1"]
    if s == 5:
        uses += [f"v{i}" for i in range(2 * T)] + ["q0", "k0", "m0a", "m0b"]
        for m in range(1, NP):
            uses += [f"q{m}", f"k{m}", f"m{m}a", f"m{m}b"]
        return uses + ["y0", "y1"]
    if s == 0:
        uses += ["c0", "c1"]
    uses += ["q0", "q1", "k0", "k1", "v0", "v1", "m0", "m1", "r0", "m2", "r1", "m3", "r2", "r3", "y0", "y1"]
    if s in MLP:
        uses += ["h0", "h1"] + [f"f{m}" for m in range(FC)] + ["z0", "z1"]
    return uses


USES = [small_uses(s) for s in STAGES]

VECS = {}
for _s in STAGES:
    VECS[f"g{_s}"] = VECS[f"b{_s}"] = C
for _n in ("gc", "bc"):
    VECS[_n] = C
for _s in BIASED:
    VECS[f"qb{_s}"] = VECS[f"kb{_s}"] = C
for _s in MLP:
    VECS[f"gm{_s}"] = VECS[f"bm{_s}"] = C
    VECS[f"f{_s}"] = FC
VCOL, _at = {}, 0
for _n, _k in VECS.items():
    VCOL[_n] = _at
    _at += _k
NVEC = _at
ROWS_B = ["o0", "o1", "o2", "o3", "o4", "z0", "z2", "z4", "v1", "v2"]


def per_unit(s):
    a = 1 if s < 5 else 0
    n = NORMS[s]
    return {
        "x_in": 16, "x_out": 16, "ctx_in": 16 if s not in OWN_KEYS else 0, "mask_in": 32 if s == 0 else 0,
        "pens": 1 if s == 0 else 0,
        "stats": n, "moments": n, "variance": n if s < 5 else 3, "rstd": n, "normed": n,
        "biased": 2 if s in MLP else a, "high": 4 * a, "mid": 4 * a, "low": 4 * a,
        "q_stacked": 96 * a, "k_stacked": 96 * a,
        "s_full": 16 * G * a or 8 * NP, "s_read": 16 * G * a or 8 * NP,
        "split": 4 * G * a, "rows_in0": 32 * a, "rows_in1": 32 * a,
        "st_full": 16 * G * a or 8 * NP, "exp_done": 16 * G * a or 8 * NP,
        "pv_done": 4 * G * a or 4 * NP, "o_out": G * a or NP, "o_scaled": (G if s != 2 else 2 * G) * a or NP,
        "low5": 2 * NP if s == 5 else 0,
        "small_full0": len(USES[s]) // 2, "small_full1": len(USES[s]) // 2,
        "small_read0": len(USES[s]) // 2, "small_read1": len(USES[s]) // 2,
    }


PER = [per_unit(s) for s in STAGES]
AHEAD = {"small_read0": 1, "small_read1": 1, "x_out": 16}


def build(nc, x, ctx, ctxT, maskB, maskBT, maskS, maskST, vecs, rows, wa, wm1, wm2, w5, eye, pick, tri, triT, out):
    with ExitStack() as stack:
        def sb(name, shape, dt=F32):
            return stack.enter_context(nc.sbuf_tensor(name, shape, dt))

        def ps(name, shape):
            return stack.enter_context(nc.psum_tensor(name, shape, F32))

        names = list(PER[0])
        sem = {n: stack.enter_context(nc.semaphore(n)) for n in names}
        consts_in = stack.enter_context(nc.semaphore("consts_in"))
        consts_set = stack.enter_context(nc.semaphore("consts_set"))
        wa_in = [stack.enter_context(nc.semaphore(f"wa_in{i}")) for i in range(2)]
        wm_in = stack.enter_context(nc.semaphore("wm_in"))
        w5_in = stack.enter_context(nc.semaphore("w5_in"))
        maskS_in = stack.enter_context(nc.semaphore("maskS_in"))
        pensS = stack.enter_context(nc.semaphore("pensS"))
        ones_row = stack.enter_context(nc.semaphore("ones_row"))
        counted = stack.enter_context(nc.semaphore("counted"))
        valid_set = stack.enter_context(nc.semaphore("valid_set"))

        def count(name, s, b, k):
            before = B * sum(PER[i][name] for i in range(s)) + AHEAD.get(name, 0)
            return b * PER[s][name] + (before + k)

        def bank(s, use):
            return USES[s].index(use) % 2

        def full(s, use):
            return sem[f"small_full{bank(s, use)}"]

        def read(s, use):
            return sem[f"small_read{bank(s, use)}"]

        def full_at(s, b, use):
            return count(f"small_full{bank(s, use)}", s, b, USES[s].index(use) // 2 + 1)

        def free_at(s, b, use):
            return count(f"small_read{bank(s, use)}", s, b, USES[s].index(use) // 2)

        def read_at(s, b, use):
            return free_at(s, b, use) + 1

        x_all = sb("x_all", [P, B, T * D])
        xw = sb("xw", [P, T, D])
        xn = sb("xn", [P, T, D])
        hT = sb("hT", [P, C, S])
        cT = sb("cT", [P, C, S])
        stats = sb("stats", [P, T, 6])
        mom = sb("mom", [P, T, 2])
        var = sb("var", [P, 3, T])
        rstd = sb("rstd", [P, T])
        eps = sb("eps", [P, 2, T])
        mhalf = sb("mhalf", [P, T])
        zero = sb("zero", [P, 16])
        scratch = sb("scratch", [P, 4])
        parts = sb("parts", [P, 2, 3, C * S], BF16)
        rest = sb("rest", [P, 2, C, S])
        Qs = sb("Qs", [P, H, S], BF16)
        Ks = sb("Ks", [P, H, S], BF16)
        V = sb("V", [P, T, H, 32])
        probs = sb("probs", [P, 2, 4, S])
        oT = sb("oT", [P, 2, S])
        recip = sb("recip", [P, 2, S])
        oN = sb("oN", [P, G, S])
        cw = recip[:].rearrange("p k n -> p (k n)").rearrange("p (t d) -> p t d", t=T)
        cn = oN[:].rearrange("p g n -> p (g n)")[:, 0:T * D].rearrange("p (t d) -> p t d", t=T)
        nmax = sb("nmax", [P, 2, T, 4])
        nrest = sb("nrest", [P, 2, T, 4])
        nparts = sb("nparts", [P, 2, T, 3, 4], BF16)
        nrows = sb("nrows", [12, 2, S], BF16)
        masks = sb("masks", [P, 2, T * S], U8)
        pens = sb("pens_sb", [P, 2, T * S], BF16)
        valid = sb("valid", [P, S])
        vtmp = oT[:, 0, :]
        WA = sb("WA", [P, 2, 3 * C * D + G * D])
        W1 = sb("W1", [P, C, FF])
        W2 = sb("W2", [P, FC, D])
        gel = Qs[:].rearrange("p a b -> p (a b)").bitcast(F32).rearrange("p (m n) -> p m n", m=FC)
        vec = sb("vec", [P, NVEC])
        row = sb("row", [P, len(ROWS_B), D])
        ident = sb("ident", [P, P])
        identb = sb("identb", [P, P], BF16)
        onesb = sb("onesb", [P, P], BF16)
        pickf = sb("pickf", [P, P])
        ones64 = sb("ones64", [P, DL])
        trib = sb("trib", [P, 2, P], BF16)
        trif = sb("trif", [P, 2, P])
        Wq5, Wk5 = W1, W2[:].rearrange("p a b -> p (a b)").rearrange("p (c n) -> p c n", c=C)
        wa_flat = WA[:].rearrange("p a b -> p (a b)")
        Wv5 = wa_flat[:, 0:C * HL].rearrange("p (c n) -> p c n", c=C)
        Wo5 = wa_flat[:, C * HL:2 * C * HL].rearrange("p (m n) -> p m n", m=NP)
        V5 = Qs[:].rearrange("p a b -> p (a b)").bitcast(F32).rearrange("p (t n) -> p t n", t=T)
        o5 = Ks[:].rearrange("p a b -> p (a b)").bitcast(F32).rearrange("p (m n) -> p m n", m=NP)
        Q5 = oN[0:DL + 1].rearrange("p (a j) n -> p a j n", a=2)
        K5 = rest[0:DL + 1]
        qb5 = parts[:].rearrange("p a b c -> p (a b c)")[0:DL, 0:4 * S].rearrange("p (a j n) -> p a j n", a=2, j=2)
        kb5 = parts[:].rearrange("p a b c -> p (a b c)")[0:DL, 4 * S:8 * S].rearrange("p (a j n) -> p a j n", a=2, j=2)

        def weights(s):
            w = WA[:, s % 2, :]
            n = C * D
            return (*(w[:, i * n:(i + 1) * n].rearrange("p (c n) -> p c n", c=C) for i in range(3)),
                    w[:, 3 * n:].rearrange("p (g n) -> p g n", g=G))

        def v_(name, i=0):
            return vec[:, VCOL[name] + i:VCOL[name] + i + 1]

        psS = [ps(f"psS{i}", [P, S]) for i in range(2)]
        psT = [ps(f"psT{i}", [P, S]) for i in range(3)]
        psO = ps("psO", [P, S])
        small = [ps(f"small{i}", [P, S]) for i in range(2)]

        def sm(s, use):
            return small[bank(s, use)]

        block = stack.enter_context(nc.Block())

        @block.sync
        def _(sp):
            for dst, src in ((vec[:], vecs), (row[:], rows), (ident[:], eye), (pickf[:], pick),
                             (trif[:, 0, :], tri), (trif[:, 1, :], triT)):
                sp.dma_start(dst, src).then_inc(consts_in, 16)
            sp.dma_start(WA[:, 0, :], wa[0]).then_inc(wa_in[0], 16)
            sp.dma_start(W1[:], wm1[0]).then_inc(wm_in, 16)
            sp.dma_start(W2[:], wm2[0]).then_inc(wm_in, 16)

            def unit_end(s, b):
                sp.wait_ge(read(s, ("z" if s in MLP else "y") + "1"), read_at(s, b, ("z" if s in MLP else "y") + "1"))
                dst = out[b].rearrange("(t p) d -> p t d", p=P) if s == 5 else \
                    x_all[:, b, :].rearrange("p (t d) -> p t d", t=T)
                sp.dma_start(dst, xw[:]).then_inc(sem["x_out"], 16)

            for s in STAGES:
                if s < 4:
                    sp.dma_start(WA[:, (s + 1) % 2, :], wa[s + 1]).then_inc(wa_in[(s + 1) % 2], 16)
                if s in (1, 3):
                    sp.dma_start(W1[:], wm1[(s + 1) // 2]).then_inc(wm_in, 16)
                    sp.dma_start(W2[:], wm2[(s + 1) // 2]).then_inc(wm_in, 16)
                if s == 2:
                    sp.dma_start(masks[:, 0, :].rearrange("p (t n) -> p t n", t=T),
                                 maskS.rearrange("(t p) n -> p t n", p=P)).then_inc(maskS_in, 16)
                    sp.dma_start(masks[:, 1, :].rearrange("p (t n) -> p t n", t=T),
                                 maskST.rearrange("(t p) n -> p t n", p=P)).then_inc(maskS_in, 16)
                if s == 5:
                    for i, dst in enumerate((Wq5[:], Wk5, Wv5, Wo5)):
                        sp.dma_start(dst, w5[i].rearrange("p (c n) -> p c n", c=NP if i == 3 else C)).then_inc(w5_in, 16)
                with sp.Fori(0, B) as b:
                    src = x[b].rearrange("(t p) d -> p t d", p=P) if s == 0 else \
                        x_all[:, b, :].rearrange("p (t d) -> p t d", t=T)
                    sp.wait_ge(sem["x_out"], count("x_out", s, b, 0))
                    sp.dma_start(xw[:], src).then_inc(sem["x_in"], 16)
                    if s == 0:
                        sp.dma_start(cw[:], ctx[b].rearrange("(t p) d -> p t d", p=P)).then_inc(sem["ctx_in"], 16)
                        for i, m in enumerate((maskB, maskBT)):
                            sp.dma_start(masks[:, i, :].rearrange("p (t n) -> p t n", t=T),
                                         m[b].rearrange("(t p) n -> p t n", p=P)).then_inc(sem["mask_in"], 16)
                    elif s not in OWN_KEYS:
                        sp.dma_start(cT[:], ctxT[b].rearrange("(c p) n -> p c n", p=P)).then_inc(sem["ctx_in"], 16)
                    if s < 5:
                        for i, (dst, slots, done) in enumerate(((Qs, Q_SLOTS, "q_stacked"), (Ks, K_SLOTS, "k_stacked"))):
                            sp.wait_ge(sem["low"], count("low", s, b, 2 * i + 2))
                            for k, part in enumerate(slots):
                                sp.dma_start(dst[DH * k:DH * (k + 1), :, :], parts[:, i, part, :]).then_inc(sem[done], 16)
                        for g in range(G):
                            sp.wait_ge(read(s, f"m{g}"), read_at(s, b, f"m{g}"))
                            sp.dma_start(Qs[ROWS:KROWS, 4 * g:4 * g + 4, :], nrows[:, g % 2, :]).then_inc(sem[f"rows_in{g % 2}"], 16)
                    unit_end(s, b)

            sp.wait_ge(sem["x_out"], AHEAD["x_out"] + 16 * B * len(STAGES))

        @block.tensor
        def _(pe):
            def transposes(s, b, letter, src):
                for c in range(C):
                    use = f"{letter}{c}"
                    pe.wait_ge(read(s, use), free_at(s, b, use))
                    for t in range(T):
                        last = nc.tensor.transpose(sm(s, use)[:, t * P:(t + 1) * P], src[:, t, c * P:(c + 1) * P], ident[:])
                    last.then_inc(full(s, use), 1)

            def projection(s, b, use, w, cols, src):
                pe.wait_ge(read(s, use), free_at(s, b, use))
                for c in range(C):
                    last = nc.tensor.matmul(sm(s, use)[:], w[:, c, cols], src[:, c, :], start=c == 0, stop=c == C - 1)
                last.then_inc(full(s, use), 1)

            def token_major(s, b, use, i, src, n, w):
                pe.wait_ge(read(s, use), free_at(s, b, use))
                for t in (2 * i, 2 * i + 1):
                    for c in range(n):
                        last = nc.tensor.matmul(sm(s, use)[:, (t % 2) * D:(t % 2 + 1) * D], src[:, c, t * P:(t + 1) * P],
                                                w[:, c, :], start=c == 0, stop=c == n - 1)
                last.then_inc(full(s, use), 1)

            def mlp(s, b):
                pe.wait_ge(sem["normed"], count("normed", s, b, NORMS[s]))
                transposes(s, b, "h", xn)
                pe.wait_ge(read(s, "h0"), read_at(s, b, "h0"))
                pe.wait_ge(read(s, "h1"), read_at(s, b, "h1"))
                for m in range(FC):
                    projection(s, b, f"f{m}", W1, slice(m * P, (m + 1) * P), hT)
                pe.wait_ge(read(s, f"f{FC - 2}"), read_at(s, b, f"f{FC - 2}"))
                pe.wait_ge(read(s, f"f{FC - 1}"), read_at(s, b, f"f{FC - 1}"))
                for i in range(2):
                    token_major(s, b, f"z{i}", i, gel, FC, W2)

            def unit(s, b):
                wq, wk, wv, wo = weights(s)
                keys = hT if s in OWN_KEYS else cT
                pe.wait_ge(sem["normed"], count("normed", s, b, 1))
                transposes(s, b, "x", xn)
                if s == 0:
                    pe.wait_ge(sem["normed"], count("normed", s, b, 2))
                    transposes(s, b, "c", cn)
                pe.wait_ge(read(s, "x0"), read_at(s, b, "x0"))
                pe.wait_ge(read(s, "x1"), read_at(s, b, "x1"))
                for c in range(C):
                    projection(s, b, f"q{c}", wq, slice(c * P, (c + 1) * P), hT)
                if s == 0:
                    pe.wait_ge(read(s, "c0"), read_at(s, b, "c0"))
                    pe.wait_ge(read(s, "c1"), read_at(s, b, "c1"))
                elif s not in OWN_KEYS:
                    pe.wait_ge(sem["ctx_in"], count("ctx_in", s, b, 16))
                for c in range(C):
                    projection(s, b, f"k{c}", wk, slice(c * P, (c + 1) * P), keys)
                for i in range(2):
                    token_major(s, b, f"v{i}", i, keys, C, wv)
                pe.wait_ge(sem["q_stacked"], count("q_stacked", s, b, 96))
                pe.wait_ge(sem["k_stacked"], count("k_stacked", s, b, 96))
                if s == 0:
                    pe.wait_ge(sem["pens"], count("pens", s, b, 1))

                def max_scores(i, j):
                    g, qt = divmod(i, T)
                    h = 4 * g + j
                    n = (qt + 1) * P if s == CAUSAL else S
                    if 4 * i + j >= 2:
                        pe.wait_ge(sem["s_read"], count("s_read", s, b, 4 * i + j - 1))
                    dst = psS[j % 2]
                    last = nc.tensor.matmul(dst[:, 0:n], Qs[0:ROWS, h, qt * P:(qt + 1) * P], Ks[0:ROWS, h, 0:n],
                                            start=True, stop=s not in (*MASKED, CAUSAL))
                    if s in MASKED:
                        last = nc.tensor.matmul(dst[:], identb[:], pens[:, 0, qt * S:(qt + 1) * S], start=False, stop=True)
                    if s == CAUSAL:
                        last = nc.tensor.matmul(dst[:, n - P:n], identb[:], trib[:, 0, :], start=False, stop=True)
                    last.then_inc(sem["s_full"], 1)

                def exp_scores(i, j):
                    g, kt = divmod(i, T)
                    h = 4 * g + j
                    at = 4 * i + j
                    q0 = kt * P if s == CAUSAL else 0
                    if i % T == 0 and j == 0:
                        pe.wait_ge(sem[f"rows_in{g % 2}"], count(f"rows_in{g % 2}", s, b, 16 * (g // 2 + 1)))
                    if at >= 3:
                        pe.wait_ge(sem["exp_done"], count("exp_done", s, b, at - 2))
                    dst = psT[at % 3]
                    last = nc.tensor.matmul(dst[:, q0:S], Ks[0:KROWS, h, kt * P:(kt + 1) * P], Qs[0:KROWS, h, q0:S],
                                            start=True, stop=s not in (*MASKED, CAUSAL))
                    if s in MASKED:
                        last = nc.tensor.matmul(dst[:], identb[:], pens[:, 1, kt * S:(kt + 1) * S], start=False, stop=True)
                    if s == CAUSAL:
                        last = nc.tensor.matmul(dst[:, q0:q0 + P], identb[:], trib[:, 1, :], start=False, stop=True)
                    last.then_inc(sem["st_full"], 1)

                def outputs(i):
                    g, kt = divmod(i, T)
                    q0 = kt * P if s == CAUSAL else 0
                    pe.wait_ge(sem["exp_done"], count("exp_done", s, b, 4 * i + 4))
                    if kt == 0 and g:
                        pe.wait_ge(sem["o_out"], count("o_out", s, b, g))
                    for j in range(4):
                        last = nc.tensor.matmul(psO[32 * j:32 * j + 32, q0:S], V[:, kt, 4 * g + j, :], probs[:, i % 2, j, q0:S],
                                                start=kt == 0, stop=kt == T - 1)
                    last.then_inc(sem["pv_done"], 1)

                def max_rows(g):
                    use = f"m{g}"
                    pe.wait_ge(sem["split"], count("split", s, b, 4 * (g + 1)))
                    pe.wait_ge(read(s, use), free_at(s, b, use))
                    for qt in range(T):
                        last = nc.tensor.matmul(sm(s, use)[0:12, qt * P:(qt + 1) * P],
                                                nparts[:, g % 2, qt, :, :].rearrange("p a b -> p (a b)"), identb[:],
                                                start=True, stop=True)
                    last.then_inc(full(s, use), 1)

                def sums(g):
                    use = f"r{g}"
                    pe.wait_ge(sem["o_out"], count("o_out", s, b, g + 1))
                    pe.wait_ge(read(s, use), free_at(s, b, use))
                    nc.tensor.matmul(sm(s, use)[:], pickf[:], oT[:, g % 2, :], start=True, stop=True).then_inc(full(s, use), 1)

                steps = G * T
                for i in range(-LEAD, steps + 1):
                    for j in range(4):
                        if i + LEAD < steps:
                            max_scores(i + LEAD, j)
                        if 0 <= i < steps:
                            exp_scores(i, j)
                    if i >= 1:
                        outputs(i - 1)
                    if i % T == 1 and i > 1:
                        sums(i // T - 1)
                    if (i + 2) % T == 0 and -2 <= i < steps - 2:
                        max_rows((i + 2) // T)
                sums(G - 1)
                pe.wait_ge(sem["o_scaled"], count("o_scaled", s, b, PER[s]["o_scaled"]))
                for i in range(2):
                    token_major(s, b, f"y{i}", i, oN, G, wo)
                if s in MLP:
                    mlp(s, b)

            def last_unit(b):
                s = 5
                pe.wait_ge(sem["normed"], count("normed", s, b, 1))
                transposes(s, b, "x", xn)
                pe.wait_ge(sem["ctx_in"], count("ctx_in", s, b, 16))
                for i in range(2 * T):
                    t, half = divmod(i, 2)
                    pe.wait_ge(read(s, f"v{i}"), free_at(s, b, f"v{i}"))
                    for c in range(C):
                        last = nc.tensor.matmul(sm(s, f"v{i}")[:], cT[:, c, t * P:(t + 1) * P], Wv5[:, c, half * S:(half + 1) * S],
                                                start=c == 0, stop=c == C - 1)
                    last.then_inc(full(s, f"v{i}"), 1)
                pe.wait_ge(read(s, "x0"), read_at(s, b, "x0"))
                pe.wait_ge(read(s, "x1"), read_at(s, b, "x1"))

                def project(m, letter):
                    projection(s, b, f"{letter}{m}", Wq5 if letter == "q" else Wk5, slice(m * P, (m + 1) * P),
                               hT if letter == "q" else cT)

                def max_scores(m, qt):
                    if qt == 0:
                        pe.wait_ge(sem["low5"], count("low5", s, b, 2 * m + 2))
                    for j in range(2):
                        at = 8 * m + 2 * qt + j
                        if at >= 2:
                            pe.wait_ge(sem["s_read"], count("s_read", s, b, at - 1))
                        nc.tensor.matmul(psS[j][:], qb5[:, m % 2, j, qt * P:(qt + 1) * P], kb5[:, m % 2, j, :],
                                         start=True, stop=True).then_inc(sem["s_full"], 1)

                def max_rows(m):
                    pe.wait_ge(sem["s_read"], count("s_read", s, b, 8 * m + 8))
                    for j in range(2):
                        use = f"m{m}" + "ab"[j]
                        pe.wait_ge(read(s, use), free_at(s, b, use))
                        for qt in range(T):
                            last = nc.tensor.matmul(sm(s, use)[DL:DL + 1, qt * P:(qt + 1) * P], nmax[:, m % 2, qt, j:j + 1],
                                                    ident[:], start=True, stop=True)
                        last.then_inc(full(s, use), 1)

                def exp_scores(m, kt):
                    for j in range(2):
                        at = 8 * m + 2 * kt + j
                        if kt == 0:
                            pe.wait_ge(read(s, f"m{m}" + "ab"[j]), read_at(s, b, f"m{m}" + "ab"[j]))
                        if at >= 2:
                            pe.wait_ge(sem["exp_done"], count("exp_done", s, b, at - 1))
                        nc.tensor.matmul(psT[j][:], K5[:, m % 2, j, kt * P:(kt + 1) * P], Q5[:, m % 2, j, :],
                                         start=True, stop=True).then_inc(sem["st_full"], 1)

                def outputs(m, kt):
                    pe.wait_ge(sem["exp_done"], count("exp_done", s, b, 8 * m + 2 * kt + 2))
                    if kt == 0 and m:
                        pe.wait_ge(sem["o_scaled"], count("o_scaled", s, b, m))
                    for j in range(2):
                        h = 2 * m + j
                        nc.tensor.matmul(psO[DL * j:DL * (j + 1), :], V5[:, kt, h * DL:(h + 1) * DL], probs[:, kt % 2, j, :],
                                         start=kt == 0, stop=kt == T - 1)
                    for j in range(2):
                        last = nc.tensor.matmul(psT[2][DL * j:DL * (j + 1), :], ones64[:], probs[:, kt % 2, j, :],
                                                start=kt == 0, stop=kt == T - 1)
                    last.then_inc(sem["pv_done"], 1)

                project(0, "q")
                project(0, "k")
                for qt in range(T):
                    max_scores(0, qt)
                max_rows(0)
                for m in range(NP):
                    for kt in range(T):
                        exp_scores(m, kt)
                        if m + 1 < NP:
                            if kt < 2:
                                project(m + 1, "qk"[kt])
                            else:
                                max_scores(m + 1, 2 * kt - 4)
                                max_scores(m + 1, 2 * kt - 3)
                        outputs(m, kt)
                    if m + 1 < NP:
                        max_rows(m + 1)
                pe.wait_ge(sem["o_scaled"], count("o_scaled", s, b, NP))
                for i in range(2):
                    token_major(s, b, f"y{i}", i, o5, NP, Wo5)

            pe.wait_ge(consts_in, 16 * 6)
            pe.wait_ge(consts_set, 3)
            for s in STAGES:
                if s < 5:
                    pe.wait_ge(wa_in[s % 2], 16 * (s // 2 + 1))
                else:
                    pe.wait_ge(w5_in, 16 * 4)
                    pe.wait_ge(ones_row, 1)
                if s in MLP:
                    pe.wait_ge(wm_in, 32 * (s // 2 + 1))
                if s == 2:
                    pe.wait_ge(pensS, 1)
                    for kt in range(T):
                        last = nc.tensor.matmul(psO[:], onesb[:], pens[:, 1, kt * S:(kt + 1) * S], start=kt == 0, stop=kt == T - 1)
                    last.then_inc(counted, 1)
                    pe.wait_ge(valid_set, 4)
                with pe.Fori(0, B) as b:
                    if s < 5:
                        unit(s, b)
                    else:
                        last_unit(b)

        @block.scalar
        def _(act):
            def to_feature_major(s, b, letter, dst, gain, bias):
                for c in range(C):
                    use = f"{letter}{c}"
                    act.wait_ge(full(s, use), full_at(s, b, use))
                    nc.scalar.activation(dst[:, c, :], sm(s, use)[:], ACT.Identity, bias=v_(bias, c) if bias else 0.0,
                                         scale=v_(gain, c)).then_inc(read(s, use), 1)

            def make_pens():
                return nc.scalar.activation(pens[:], masks[:], ACT.Copy, scale=-BIG)

            def unit(s, b):
                to_feature_major(s, b, "x", hT, f"g{s}", f"b{s}")
                if s == 0:
                    to_feature_major(s, b, "c", cT, "gc", "bc")
                for i, letter in enumerate("qk"):
                    for c in range(C):
                        use = f"{letter}{c}"
                        n = 2 * i + c
                        act.wait_ge(full(s, use), full_at(s, b, use))
                        bias = v_(f"{letter}b{s}", c) if s in BIASED else 0.0
                        nc.scalar.activation(parts[:, i, 0, c * S:(c + 1) * S], sm(s, use)[:], ACT.Identity, bias=bias)\
                            .then_inc(sem["high"], 1)
                        act.wait_ge(read(s, use), read_at(s, b, use))
                        nc.scalar.activation(parts[:, i, 1, c * S:(c + 1) * S], rest[:, i, c, :], ACT.Copy).then_inc(sem["mid"], 1)
                if s == 0:
                    act.wait_ge(sem["mask_in"], count("mask_in", s, b, 32))
                    make_pens().then_inc(sem["pens"], 1)

                def max_rows(g):
                    act.wait_ge(full(s, f"m{g}"), full_at(s, b, f"m{g}"))
                    nc.scalar.activation(nrows[:, g % 2, :], sm(s, f"m{g}")[0:12, :], ACT.Copy).then_inc(read(s, f"m{g}"), 1)

                def take_outputs(g):
                    act.wait_ge(sem["pv_done"], count("pv_done", s, b, T * (g + 1)))
                    if g >= 2:
                        act.wait_ge(sem["o_scaled"], count("o_scaled", s, b, (g - 1) * PER[s]["o_scaled"] // G))
                    nc.scalar.activation(oT[:, g % 2, :], psO[:], ACT.Copy).then_inc(sem["o_out"], 1)

                steps = G * T
                max_rows(0)
                for i in range(steps):
                    kt = i % T
                    q0 = kt * P if s == CAUSAL else 0
                    for j in range(4):
                        at = 4 * i + j
                        act.wait_ge(sem["st_full"], count("st_full", s, b, at + 1))
                        if i >= 2 and j == 0:
                            act.wait_ge(sem["pv_done"], count("pv_done", s, b, i - 1))
                        nc.scalar.activation(probs[:, i % 2, j, q0:S], psT[at % 3][:, q0:S], ACT.Exp, scale=float(DH) ** -0.5)\
                            .then_inc(sem["exp_done"], 1)
                        if j == 1 and kt == 0 and i:
                            take_outputs(i // T - 1)
                    if (i + 2) % T == 0 and -2 <= i < steps - 2:
                        max_rows((i + 2) // T)
                take_outputs(G - 1)
                if s in MLP:
                    to_feature_major(s, b, "h", hT, f"gm{s}", f"bm{s}")
                    for m in range(FC):
                        act.wait_ge(full(s, f"f{m}"), full_at(s, b, f"f{m}"))
                        nc.scalar.activation(gel[:, m, :], sm(s, f"f{m}")[:], ACT.Gelu, bias=v_(f"f{s}", m)).then_inc(read(s, f"f{m}"), 1)

            def last_unit(b):
                s = 5
                to_feature_major(s, b, "x", hT, "g5", None)
                for i in range(0, 2 * T, 2):
                    act.wait_ge(full(s, f"v{i}"), full_at(s, b, f"v{i}"))
                    nc.scalar.activation(V5[:, i // 2, 0:S], sm(s, f"v{i}")[:], ACT.Copy).then_inc(read(s, f"v{i}"), 1)

                def even_head(m, letter):
                    use = f"{letter}{m}"
                    act.wait_ge(full(s, use), full_at(s, b, use))
                    dst, low = (Q5, qb5) if letter == "q" else (K5, kb5)
                    nc.scalar.activation(dst[0:DL, m % 2, 0, :], sm(s, use)[0:DL, :], ACT.Copy)
                    nc.scalar.activation(low[:, m % 2, 0, :], sm(s, use)[0:DL, :], ACT.Copy)
                    nc.scalar.activation(low[:, m % 2, 1, :], sm(s, use)[DL:P, :], ACT.Copy).then_inc(sem["low5"], 1)

                def max_rows(m):
                    for j in range(2):
                        use = f"m{m}" + "ab"[j]
                        act.wait_ge(full(s, use), full_at(s, b, use))
                        nc.scalar.activation(Q5[DL:DL + 1, m % 2, j, :], sm(s, use)[DL:DL + 1, :], ACT.Copy).then_inc(read(s, use), 1)

                even_head(0, "q")
                even_head(0, "k")
                max_rows(0)
                for m in range(NP):
                    for kt in range(T):
                        for j in range(2):
                            at = 8 * m + 2 * kt + j
                            act.wait_ge(sem["st_full"], count("st_full", s, b, at + 1))
                            if 4 * m + kt >= 2 and j == 0:
                                act.wait_ge(sem["pv_done"], count("pv_done", s, b, 4 * m + kt - 1))
                            nc.scalar.activation(probs[:, kt % 2, j, :], psT[j][:], ACT.Exp).then_inc(sem["exp_done"], 1)
                        if m + 1 < NP and kt < 2:
                            even_head(m + 1, "qk"[kt])
                    if m + 1 < NP:
                        max_rows(m + 1)

            act.wait_ge(consts_in, 16 * 6)
            nc.scalar.activation(identb[:], ident[:], ACT.Copy)
            nc.scalar.activation(trib[:], trif[:], ACT.Copy).then_inc(consts_set, 1)
            for s in STAGES:
                if s == 2:
                    act.wait_ge(maskS_in, 32)
                    make_pens().then_inc(pensS, 1)
                with act.Fori(0, B) as b:
                    if s < 5:
                        unit(s, b)
                    else:
                        last_unit(b)

        @block.vector
        def _(dve):
            def moments(s, b, n, src):
                for t in range(T):
                    last = nc.vector.bn_stats(stats[:, t, :], src[:, t, :])
                last.then_inc(sem["stats"], 1)
                dve.wait_ge(sem["stats"], count("stats", s, b, n))
                nc.vector.memset(scratch[:, 3:4], 0.0)
                for t in range(T):
                    last = nc.vector.bn_aggr(mom[:, t, :], stats[:, t, :])
                last.then_inc(sem["moments"], 1)

            def normalise(s, b, n, src, dst):
                dve.wait_ge(sem["rstd"], count("rstd", s, b, n))
                for t in range(T):
                    if s == 5:
                        last = nc.vector.tensor_scalar(dst[:, t, :], src[:, t, :], rstd[:, t:t + 1], None, ALU.mult)
                    else:
                        last = nc.vector.tensor_scalar(dst[:, t, :], src[:, t, :], mom[:, t, 0:1], rstd[:, t:t + 1],
                                                       ALU.subtract, ALU.mult)
                last.then_inc(sem["normed"], 1)

            def add_to_x(s, b, letter, n):
                for i in range(2):
                    use = f"{letter}{i}"
                    if n and i == 0:
                        dve.wait_ge(sem["biased"], count("biased", s, b, n))
                    dve.wait_ge(full(s, use), full_at(s, b, use))
                    xs = xw[:, 2 * i:2 * i + 2, :]
                    nc.vector.tensor_tensor(xs, xs, sm(s, use)[:].rearrange("p (t n) -> p t n", t=2), ALU.add).then_inc(read(s, use), 1)

            def unit(s, b):
                dve.wait_ge(sem["x_in"], count("x_in", s, b, 16))
                moments(s, b, 1, xw)
                normalise(s, b, 1, xw, xn)
                if s == 0:
                    dve.wait_ge(sem["ctx_in"], count("ctx_in", s, b, 16))
                    moments(s, b, 2, cw)
                    normalise(s, b, 2, cw, cn)
                for i, letter in enumerate("qk"):
                    for c in range(C):
                        use = f"{letter}{c}"
                        dve.wait_ge(sem["high"], count("high", s, b, 2 * i + c + 1))
                        high = parts[:, i, 0, c * S:(c + 1) * S]
                        if s in BIASED:
                            last = nc.vector.scalar_tensor_tensor(rest[:, i, c, :], sm(s, use)[:], v_(f"{letter}b{s}", c), high,
                                                                  ALU.add, ALU.subtract)
                        else:
                            last = nc.vector.tensor_tensor(rest[:, i, c, :], sm(s, use)[:], high, ALU.subtract)
                        last.then_inc(read(s, use), 1)
                for i in range(2):
                    use = f"v{i}"
                    dve.wait_ge(full(s, use), full_at(s, b, use))
                    dst = V[:, 2 * i:2 * i + 2, :, 0:DH]
                    src = sm(s, use)[:].rearrange("p (t h d) -> p t h d", t=2, h=H)
                    if s in BIASED:
                        for t in range(2):
                            last = nc.vector.tensor_tensor(dst[:, t], src[:, t],
                                                           row[:, ROWS_B.index(f"v{s}"), :].rearrange("p (h d) -> p h d", h=H), ALU.add)
                    else:
                        last = nc.vector.tensor_copy(dst, src)
                    last.then_inc(read(s, use), 1)

                def maximum(i, j):
                    g, qt = divmod(i, T)
                    n = (qt + 1) * P if s == CAUSAL else S
                    dve.wait_ge(sem["s_full"], count("s_full", s, b, 4 * i + j + 1))
                    nc.vector.tensor_reduce(nmax[:, g % 2, qt, j:j + 1], psS[j % 2][:, 0:n], AX, ALU.max, negate=True)\
                        .then_inc(sem["s_read"], 1)

                def reciprocals(g):
                    dve.wait_ge(full(s, f"r{g}"), full_at(s, b, f"r{g}"))
                    if g >= 2:
                        dve.wait_ge(sem["o_scaled"], count("o_scaled", s, b, (g - 1) * PER[s]["o_scaled"] // G))
                    nc.vector.reciprocal(recip[:, g % 2, :], sm(s, f"r{g}")[:]).then_inc(read(s, f"r{g}"), 1)

                steps = G * T
                for i in range(-LEAD, steps + 1):
                    if i + LEAD < steps:
                        for j in range(4):
                            maximum(i + LEAD, j)
                    if i % T == 1 and i > 1:
                        reciprocals(i // T - 1)
                reciprocals(G - 1)
                add_to_x(s, b, "y", 1)
                if s in MLP:
                    dve.wait_ge(read(s, "y0"), read_at(s, b, "y0"))
                    dve.wait_ge(read(s, "y1"), read_at(s, b, "y1"))
                    moments(s, b, NORMS[s], xw)
                    normalise(s, b, NORMS[s], xw, xn)
                    add_to_x(s, b, "z", 2)

            def last_unit(b):
                s = 5
                dve.wait_ge(sem["x_in"], count("x_in", s, b, 16))
                moments(s, b, 1, xw)
                normalise(s, b, 1, xw, xn)
                for i in range(1, 2 * T, 2):
                    dve.wait_ge(full(s, f"v{i}"), full_at(s, b, f"v{i}"))
                    nc.vector.tensor_copy(V5[:, i // 2, S:2 * S], sm(s, f"v{i}")[:]).then_inc(read(s, f"v{i}"), 1)

                def odd_head(m, letter):
                    use = f"{letter}{m}"
                    dve.wait_ge(sem["low5"], count("low5", s, b, 2 * m + (1 if letter == "q" else 2)))
                    dst = Q5 if letter == "q" else K5
                    nc.vector.tensor_copy(dst[0:DL, m % 2, 1, :], sm(s, use)[DL:P, :]).then_inc(read(s, use), 1)

                def maxima(m, qt):
                    for j in range(2):
                        dve.wait_ge(sem["s_full"], count("s_full", s, b, 8 * m + 2 * qt + j + 1))
                        nc.vector.tensor_reduce(nmax[:, m % 2, qt, j:j + 1], psS[j][:], AX, ALU.max, negate=True)\
                            .then_inc(sem["s_read"], 1)

                odd_head(0, "q")
                odd_head(0, "k")
                for qt in range(T):
                    maxima(0, qt)
                for m in range(NP):
                    for kt in range(T):
                        if m + 1 < NP:
                            if kt < 2:
                                odd_head(m + 1, "qk"[kt])
                            else:
                                maxima(m + 1, 2 * kt - 4)
                                maxima(m + 1, 2 * kt - 3)
                    dve.wait_ge(sem["pv_done"], count("pv_done", s, b, T * (m + 1)))
                    nc.vector.reciprocal(recip[:, m % 2, :], psT[2][:]).then_inc(sem["o_out"], 1)
                    dve.wait_ge(sem["o_out"], count("o_out", s, b, m + 1))
                    nc.vector.tensor_tensor(o5[:, m, :], psO[:], recip[:, m % 2, :], ALU.mult).then_inc(sem["o_scaled"], 1)
                add_to_x(s, b, "y", 0)

            nc.vector.memset(V[:], 1.0)
            nc.vector.memset(ones64[:], 1.0)
            nc.vector.memset(onesb[:], 1.0)
            nc.vector.memset(Ks[ROWS:KROWS, :, :], 1.0).then_inc(consts_set, 1)
            for n, name in enumerate(AHEAD):
                nc.vector.memset(scratch[:, n:n + 1], 0.0).then_inc(sem[name], AHEAD[name])
            for s in STAGES:
                if s == 2:
                    dve.wait_ge(counted, 1)
                    nc.vector.tensor_scalar(valid[:], psO[:], 1.0 / BIG, float(S), ALU.mult, ALU.add).then_inc(valid_set, 1)
                    dve.wait_ge(valid_set, 1)
                    nc.vector.tensor_scalar(vtmp, valid[:], 1.0, None, ALU.min).then_inc(valid_set, 1)
                    dve.wait_ge(valid_set, 2)
                    nc.vector.reciprocal(valid[:], vtmp).then_inc(valid_set, 1)
                    dve.wait_ge(valid_set, 3)
                    nc.vector.tensor_tensor(valid[:], valid[:], vtmp, ALU.mult).then_inc(valid_set, 1)
                if s == 5:
                    nc.vector.memset(K5[DL:DL + 1, :, :, :], 1.0).then_inc(ones_row, 1)
                with dve.Fori(0, B) as b:
                    if s < 5:
                        unit(s, b)
                    else:
                        last_unit(b)

        @block.gpsimd
        def _(pool):
            def rsqrt(s, b, n):
                pool.wait_ge(sem["moments"], count("moments", s, b, n))
                v = mom[:, :, 1]
                if s == 5:
                    nc.gpsimd.tensor_tensor(var[:, 1, :], mom[:, :, 0], mom[:, :, 0], ALU.mult).then_inc(sem["variance"], 1)
                    pool.wait_ge(sem["variance"], count("variance", s, b, 1))
                    nc.gpsimd.tensor_tensor(var[:, 2, :], mom[:, :, 1], var[:, 1, :], ALU.add).then_inc(sem["variance"], 1)
                    pool.wait_ge(sem["variance"], count("variance", s, b, 2))
                    v = var[:, 2, :]
                nc.gpsimd.tensor_tensor(var[:, 0, :], v, eps[:, int(s == 5), :], ALU.add).then_inc(sem["variance"], 1)
                pool.wait_ge(sem["variance"], count("variance", s, b, 3 if s == 5 else n))
                nc.gpsimd.tensor_tensor(rstd[:], var[:, 0, :], mhalf[:], ALU.pow).then_inc(sem["rstd"], 1)

            def bias_x(s, b, n, norm, name):
                pool.wait_ge(sem["normed"], count("normed", s, b, norm))
                r = row[:, ROWS_B.index(name), :]
                for t in range(T):
                    last = nc.gpsimd.tensor_tensor(xw[:, t, :], xw[:, t, :], r, ALU.add)
                last.then_inc(sem["biased"], 1)

            def unit(s, b):
                rsqrt(s, b, 1)
                if s == 0:
                    rsqrt(s, b, 2)
                for i in range(2):
                    for c in range(C):
                        pool.wait_ge(sem["mid"], count("mid", s, b, 2 * i + c + 1))
                        nc.gpsimd.tensor_tensor(parts[:, i, 2, c * S:(c + 1) * S], rest[:, i, c, :], parts[:, i, 1, c * S:(c + 1) * S], ALU.subtract).then_inc(sem["low"], 1)
                bias_x(s, b, 1, 1, f"o{s}")

                def split(g):
                    k = g % 2
                    z = zero[:].rearrange("p (t j) -> p t j", t=T)
                    pool.wait_ge(sem["s_read"], count("s_read", s, b, 16 * (g + 1)))
                    nc.gpsimd.tensor_tensor(nparts[:, k, :, 0, :], nmax[:, k], z, ALU.add).then_inc(sem["split"], 1)
                    pool.wait_ge(sem["split"], count("split", s, b, 4 * g + 1))
                    nc.gpsimd.tensor_tensor(nrest[:, k], nmax[:, k], nparts[:, k, :, 0, :], ALU.subtract).then_inc(sem["split"], 1)
                    pool.wait_ge(sem["split"], count("split", s, b, 4 * g + 2))
                    nc.gpsimd.tensor_tensor(nparts[:, k, :, 1, :], nrest[:, k], z, ALU.add).then_inc(sem["split"], 1)
                    pool.wait_ge(sem["split"], count("split", s, b, 4 * g + 3))
                    nc.gpsimd.tensor_tensor(nparts[:, k, :, 2, :], nrest[:, k], nparts[:, k, :, 1, :], ALU.subtract).then_inc(sem["split"], 1)

                def scale(g):
                    k = g % 2
                    pool.wait_ge(read(s, f"r{g}"), read_at(s, b, f"r{g}"))
                    if s == 2:
                        nc.gpsimd.tensor_tensor(recip[:, k, :], recip[:, k, :], valid[:], ALU.mult).then_inc(sem["o_scaled"], 1)
                        pool.wait_ge(sem["o_scaled"], count("o_scaled", s, b, 2 * g + 1))
                    nc.gpsimd.tensor_tensor(oN[:, g, :], oT[:, k, :], recip[:, k, :], ALU.mult).then_inc(sem["o_scaled"], 1)

                for use in USES[s]:
                    if use[0] == "m":
                        split(int(use[1]))
                    elif use[0] == "r":
                        scale(int(use[1]))
                if s in MLP:
                    rsqrt(s, b, NORMS[s])
                    bias_x(s, b, 2, NORMS[s], f"z{s}")

            nc.gpsimd.memset(eps[:, 0, :], LN_EPS)
            nc.gpsimd.memset(eps[:, 1, :], RMS_EPS)
            nc.gpsimd.memset(mhalf[:], -0.5)
            nc.gpsimd.memset(zero[:], 0.0).then_inc(consts_set, 1)
            pool.wait_ge(consts_set, 3)
            pool.wait_ge(consts_in, 16 * 6)
            for s in STAGES:
                if s == 2:
                    pool.wait_ge(valid_set, 4)
                with pool.Fori(0, B) as b:
                    if s < 5:
                        unit(s, b)
                    else:
                        rsqrt(5, b, 1)


def in_chunks(w):
    k, n = w.shape
    return w.reshape(k // P, P, n).transpose(1, 0, 2).reshape(P, -1)


def columns(v):
    return v.reshape(-1, P).T


def by_dim(w):
    n = w.ndim
    return w.reshape(*w.shape[:-1], GB, C, DH).transpose(*range(n - 1), n, n + 1, n - 1).reshape(w.shape)


def strips(w):
    o = np.zeros((G, 4, 32, w.shape[1]), w.dtype)
    o[:, :, :DH] = w.reshape(G, 4, DH, -1)
    return o.reshape(G, P, -1).transpose(1, 0, 2).reshape(P, -1)


def kernel(**inputs):
    import concourse.bacc as bacc
    from concourse.bass_utils import run_bass_kernel_spmd

    a = {k: np.asarray(v) for k, v in inputs.items()}
    L0, L1, L2, L3 = ({k[9:]: v for k, v in a.items() if k.startswith(f"L{i}_xattn_")} for i in range(4))
    qkv = L2["w_qkv"].T
    kv2 = L2["w_kv"].T
    att = [
        (L0["q_w"], L0["kv_w"][:, :D], L0["kv_w"][:, D:], L0["proj_w"]),
        (L1["ca_qw"], L1["ca_kw"], L1["ca_vw"], L1["ca_ow"]),
        (L1["sa_qw"], L1["sa_kw"], L1["sa_vw"], L1["sa_ow"]),
        (qkv[:, :D], qkv[:, D:2 * D], qkv[:, 2 * D:], L2["w_prj1"].T),
        (L2["w_q"].T, kv2[:, :D], kv2[:, D:], L2["w_prj2"].T),
    ]
    wa = np.stack([np.concatenate([in_chunks(by_dim(q)), in_chunks(by_dim(k)), in_chunks(v), strips(o)], axis=1)
                   for q, k, v, o in att])
    mlps = [(L0["fc1_w"], L0["fc2_w"]), (L1["w1"], L1["w2"]), (L2["w_fc1"].T, L2["w_fc2"].T)]
    vectors = {
        "g0": L0["qn_w"], "b0": L0["qn_b"], "gc": L0["cn_w"], "bc": L0["cn_b"],
        "g1": L1["ln1_g"], "b1": L1["ln1_b"], "g2": L1["ln2_g"], "b2": L1["ln2_b"],
        "g3": L2["ln1_g"], "b3": L2["ln1_b"], "g4": L2["ln2_g"], "b4": L2["ln2_b"],
        "g5": L3["norm_w"], "b5": L3["norm_w"],
        "qb1": by_dim(L1["ca_qb"]), "kb1": by_dim(L1["ca_kb"]), "qb2": by_dim(L1["sa_qb"]), "kb2": by_dim(L1["sa_kb"]),
        "gm0": L0["n2_w"], "bm0": L0["n2_b"], "f0": L0["fc1_b"],
        "gm2": L1["ln3_g"], "bm2": L1["ln3_b"], "f2": L1["b1"],
        "gm4": L2["ln3_g"], "bm4": L2["ln3_b"], "f4": L2["b_fc1"],
    }
    same = {"o0": L0["proj_b"], "o1": L1["ca_ob"], "o2": L1["sa_ob"], "o3": L2["b_prj1"], "o4": L2["b_prj2"],
            "z0": L0["fc2_b"], "z2": L1["b2"], "z4": L2["b_fc2"], "v1": L1["ca_vb"], "v2": L1["sa_vb"]}
    pick = np.zeros((P, P), np.float32)
    for j in range(4):
        pick[32 * j + DH, 32 * j:32 * j + 32] = 1.0
    upper = np.triu(np.full((P, P), -BIG, np.float32), 1)
    maskB, maskS = a["mask_BxSxS2_bk0"], a["mask_SxS_bk1"]
    arrays = {
        "x": a["x"], "ctx": a["ctx_1024"], "ctxT": a["ctx_1024"].transpose(0, 2, 1),
        "maskB": maskB, "maskBT": maskB.transpose(0, 2, 1), "maskS": maskS, "maskST": maskS.T,
        "vecs": np.concatenate([columns(vectors[n]) for n in VECS], axis=1),
        "rows": np.broadcast_to(np.stack([same[n] for n in ROWS_B]), (P, len(ROWS_B), D)),
        "wa": wa,
        "wm1": np.stack([in_chunks(w).reshape(P, C, FF) for w, _ in mlps]),
        "wm2": np.stack([in_chunks(w).reshape(P, FC, D) for _, w in mlps]),
        "w5": np.stack([in_chunks(L3[n]) for n in ("wq", "wk", "wv", "wo")]),
        "eye": np.eye(P, dtype=np.float32), "pick": pick, "tri": upper, "triT": upper.T,
    }
    arrays = {k: np.ascontiguousarray(v) for k, v in arrays.items()}
    nc = bacc.Bacc("TRN2", target_bir_lowering=False, num_devices=1)
    args = [nc.dram_tensor(k, v.shape, mybir.dt.from_np(v.dtype), kind="ExternalInput").ap() for k, v in arrays.items()]
    out = nc.dram_tensor("out", (B, S, D), F32, kind="ExternalOutput").ap()
    build(nc, *args, out)
    r = run_bass_kernel_spmd(nc, [arrays], core_ids=[0])
    return r.results[0]["out"]
```

```python
from contextlib import ExitStack

import numpy as np
import concourse.bass as bass
from concourse import mybir

P = 128
B = 8
S = 512
D = 256
C = D // P
T = S // P
H = 16
DH = D // H
DL = 64
HL = H * DL
FF = 4 * D
FC = FF // P
G = H // 4
STEPS = G * T
SLOTS = 2 * STEPS
GB = P // DH
NP = H // 2
ROWS = 6 * DH
KROWS = ROWS + 3
BIG = 2.0 ** 100
LEAD = 6
LN_EPS, RMS_EPS = 1e-5, 1e-6

F32 = mybir.dt.float32
BF16 = mybir.dt.bfloat16
U8 = mybir.dt.uint8
ALU = mybir.AluOpType
ACT = mybir.ActivationFunctionType
AX = mybir.AxisListType.X

STAGES = range(6)
OWN_KEYS = (2, 3)
MASKED = (0, 2)
CAUSAL = 3
BIASED = (1, 2)
MLP = (0, 2, 4)

Q_SLOTS = (0, 0, 0, 1, 1, 2)
K_SLOTS = (0, 1, 2, 0, 1, 0)

CUR_USES = {"m1": 5, "s0": 10, "r0": 12, "m2": 13, "s1": 18, "r1": 20, "m3": 21, "s2": 26, "r2": 28}
PREV_USES = {"s3": 2, "r3": 4, "y0": 7, "y1": 7}
MLP_USES = {"h0": 15, "h1": 15, "fa0": 17, "fa1": 17, "fa2": 19, "fa3": 19, "za": 22,
            "fb0": 23, "fb1": 23, "fb2": 25, "fb3": 25, "zb": 27}
NXT_USES = {"x0": 6, "x1": 6, "q0": 8, "q1": 10, "k0": 11, "k1": 12, "v0": 14, "v1": 14, "m0": 29}
CTX_USES = {"c0": 9, "c1": 9}
COUNT_USES = {"w": 16}


class Unit:

    def __init__(self, s, b, parity):
        self.s, self.b, self.parity = s, b, parity


class Body:
    def __init__(self, prev, cur, nxt, count_masks=False):
        self.prev, self.cur, self.nxt = prev, cur, nxt
        found = []
        if cur is not None:
            found += [(k, "cur", u) for u, k in CUR_USES.items()]
        if prev is not None:
            found += [(k, "prev", u) for u, k in PREV_USES.items()]
            if prev in MLP:
                found += [(k, "prev", u) for u, k in MLP_USES.items()]
        if nxt is not None:
            found += [(k, "nxt", u) for u, k in NXT_USES.items()]
            if nxt == 0:
                found += [(k, "nxt", u) for u, k in CTX_USES.items()]
        if count_masks:
            found += [(k, "nxt", u) for u, k in COUNT_USES.items()]
        self.uses = sorted(found, key=lambda f: f[0])
        self.order = {(who, u): i for i, (_, who, u) in enumerate(self.uses)}

    def at(self, slot):
        return [(who, u) for k, who, u in self.uses if k == slot]


def last_uses():
    uses = ["x0", "x1"] + [f"v{i}" for i in range(2 * T)] + ["q0", "k0", "m0a", "m0b"]
    for m in range(NP):
        more = m + 1 < NP
        uses += [f"q{m + 1}"] * more + [f"s{m - 1}"] * (m > 0) + [f"k{m + 1}", f"m{m + 1}a", f"m{m + 1}b"] * more
    return uses + [f"s{NP - 1}", "y0", "y1"]


LAST = last_uses()


class Place:

    def __init__(self, body, before, step=0, i=0):
        self.body, self.before, self.step, self.i = body, before, step, i

    def bank(self, who, use):
        return (self.before + self.body.order[who, use]) % 2

    def fills(self, who, use):
        return self.i * (self.step // 2) + (self.before + self.body.order[who, use]) // 2


def schedule():
    out = [(0, [(Body(None, None, 0), None, None, 0)])]
    for s in range(5):
        out.append((0, [(Body(s - 1 if s else None, s, s), B - 1, 0, 1)]))
        out.append((B // 2 - 1, [(Body(s, s, s), o - 1, o, o + 1) for o in (1, 2)]))
        out.append((0, [(Body(s, s, s + 1 if s < 4 else None, count_masks=s == 1), B - 2, B - 1, 0)]))
    out.append((0, [(Body(4, None, None), B - 1, None, None)]))
    return out


SCHEDULE = schedule()
FIRST_LAST = sum(len(body.uses) * max(turns, 1) for turns, bodies in SCHEDULE for body, *_ in bodies)
assert len(LAST) % 2 == 0

VECS = {}
for _s in STAGES:
    VECS[f"g{_s}"] = VECS[f"b{_s}"] = C
for _n in ("gc", "bc"):
    VECS[_n] = C
for _s in BIASED:
    VECS[f"qb{_s}"] = VECS[f"kb{_s}"] = C
for _s in MLP:
    VECS[f"gm{_s}"] = VECS[f"bm{_s}"] = C
    VECS[f"f{_s}"] = FC
VCOL, _at = {}, 0
for _n, _k in VECS.items():
    VCOL[_n] = _at
    _at += _k
NVEC = _at
N_QKV = 3 * C * D + D
N_WO = G * D + 2 * D


def per_unit(s):
    a = 1 if s < 5 else 0
    mlp = 1 if s in MLP else 0
    norms = 2 if s == 0 else 1
    return {
        "x_in": 16, "xe_in": 16, "x_out": 16, "ctx_in": 16 if s not in OWN_KEYS else 0, "mask_in": 32 if s == 0 else 0,
        "pens": 2 if s == 0 else 0,
        "stats": norms, "moments": norms, "variance": norms if s < 5 else 3, "rstd": norms, "normed": norms,
        "stats_m": mlp, "moments_m": mlp, "variance_m": mlp, "rstd_m": mlp, "normed_m": mlp,
        "biased": (1 + mlp) * a, "high": 4 * a, "mid": 4 * a, "low": 4 * a,
        "q_stacked": 96 * a, "k_stacked": 96 * a,
        "s_full": 4 * STEPS * a or 8 * NP, "s_read": 4 * STEPS * a or 8 * NP,
        "split": 4 * G * a, "rows_in0": 32 * a, "rows_in1": 32 * a,
        "st_full": 4 * STEPS * a or 8 * NP, "exp_done": 4 * STEPS * a or 8 * NP,
        "pv_done": STEPS * a or 4 * NP, "o_out": G * a or NP, "o_scaled": G * a or NP,
        "o_valid": G if s == 2 else 0, "low5": 2 * NP if s == 5 else 0, "summed": 3 * NP if s == 5 else 0,
    }


PER = [per_unit(s) for s in STAGES]
AHEAD = {"x_out": 16, "summed": 1}


def positive(n):
    return not isinstance(n, int) or n > 0


def build(nc, x, ctx, ctxT, maskB, maskBT, maskS, maskST, vecs, wa, wm1, wm2, w5, eye, pick, tri, triT, out):
    with ExitStack() as stack:
        def sb(name, shape, dt=F32):
            return stack.enter_context(nc.sbuf_tensor(name, shape, dt))

        def ps(name, shape):
            return stack.enter_context(nc.psum_tensor(name, shape, F32))

        def semaphore(name):
            return stack.enter_context(nc.semaphore(name))

        sem = {n: semaphore(n) for n in PER[0]}
        small_full = [semaphore(f"small_full{i}") for i in range(2)]
        small_read = [semaphore(f"small_read{i}") for i in range(2)]
        consts_in = semaphore("consts_in")
        consts_set = semaphore("consts_set")
        qkv_in = semaphore("qkv_in")
        wo_in = semaphore("wo_in")
        wm_in = semaphore("wm_in")
        w5_in = semaphore("w5_in")
        maskS_in = semaphore("maskS_in")
        pensS = semaphore("pensS")
        valid_set = semaphore("valid_set")
        ones_row = semaphore("ones_row")

        def count(name, u, k):
            return u.b * PER[u.s][name] + (AHEAD.get(name, 0) + B * sum(PER[i][name] for i in range(u.s)) + k)

        def walk(eng, run):
            before = 0
            for turns, bodies in SCHEDULE:
                step = sum(len(body.uses) for body, *_ in bodies)
                assert not turns or step % 2 == 0

                def one_turn(i, before):
                    for body, *bs in bodies:
                        units = [None if st is None else Unit(st, 2 * i + o if turns else o, o % 2)
                                 for st, o in zip((body.prev, body.cur, body.nxt), bs)]
                        run(Place(body, before, step if turns else 0, i), *units)
                        before += len(body.uses)

                if turns:
                    with eng.Fori(0, turns) as i:
                        one_turn(i, before)
                else:
                    one_turn(0, before)
                before += step * max(turns, 1)
                yield
            assert before == FIRST_LAST

        def last_bank(use):
            return (FIRST_LAST + LAST.index(use)) % 2

        def last_fills(b, use):
            return b * (len(LAST) // 2) + (FIRST_LAST + LAST.index(use)) // 2

        x_mid = nc.dram_tensor("x_mid", (B, S, D), F32).ap()

        xw = sb("xw", [P, T, D])
        xe = sb("xe", [P, T, D])
        xn = sb("xn", [P, T, D])
        hT = sb("hT", [P, C, S])
        cT = sb("cT", [P, C, S])
        gel = sb("gel", [P, FC, S // 2])
        gel_flat = gel[:].rearrange("p m n -> p (m n)")
        cw = gel_flat[:, 0:T * D].rearrange("p (t d) -> p t d", t=T)
        cn = gel_flat[:, T * D:2 * T * D].rearrange("p (t d) -> p t d", t=T)
        stats = sb("stats", [P, 2, T, 6])
        mom = sb("mom", [P, 2, T, 2])
        var = sb("var", [P, 4, T])
        rstd = sb("rstd", [P, 2, T])
        eps = sb("eps", [P, 2, T])
        mhalf = sb("mhalf", [P, T])
        zero = sb("zero", [P, 16])
        scratch = sb("scratch", [P, 4])
        parts = sb("parts", [P, 2, 3, C * S], BF16)
        rest = sb("rest", [P, 2, C, S])
        Qs = sb("Qs", [P, 2, H, S], BF16)
        Ks = sb("Ks", [P, 2, H, S], BF16)
        V = sb("V", [P, 2, T, H, 32])
        probs = sb("probs", [P, 2, 4, S])
        oT = sb("oT", [P, 2, S])
        recip = sb("recip", [P, 2, 16])
        oN = sb("oN", [P, G, S])
        nmax = sb("nmax", [P, 2, T, 4])
        nrest = sb("nrest", [P, 2, T, 4])
        nparts = sb("nparts", [P, 2, T, 3, 4], BF16)
        nrows = sb("nrows", [12, 2, S], BF16)
        masks = sb("masks", [P, 2, T * S], U8)
        pens = sb("pens_sb", [P, 2, T * S], BF16)
        valid = sb("valid", [P, S])
        vtmp = sb("vtmp", [P, S])
        Wqkv = sb("Wqkv", [P, N_QKV])
        Wo = sb("Wo", [P, N_WO])
        W1 = sb("W1", [P, C, FF])
        W2 = sb("W2", [P, FC, D])
        vec = sb("vec", [P, NVEC])
        v_row = Wqkv[:, 3 * C * D:]
        o_row, z_row = Wo[:, G * D:(G + 1) * D], Wo[:, (G + 1) * D:]
        ident = sb("ident", [P, P])
        identb = sb("identb", [P, P], BF16)
        onesb = sb("onesb", [P, P], BF16)
        pickf = sb("pickf", [P, 4])
        onesf = sb("onesf", [P, DL])
        trib = sb("trib", [P, 2, P], BF16)
        trif = probs[:, 0, 0, 0:2 * P].rearrange("p (a n) -> p a n", a=2)
        Wq5, Wk5 = W1, W2[:].rearrange("p a b -> p (a b)").rearrange("p (c n) -> p c n", c=C)
        Wv5 = pens[:].rearrange("p a b -> p (a b)").bitcast(F32).rearrange("p (c n) -> p c n", c=C)
        Wo5 = gel_flat.rearrange("p (m n) -> p m n", m=NP)
        V5 = Qs[:, 0].rearrange("p a b -> p (a b)").bitcast(F32).rearrange("p (t n) -> p t n", t=T)
        o5 = Ks[:, 0].rearrange("p a b -> p (a b)").bitcast(F32).rearrange("p (m n) -> p m n", m=NP)
        pacc = Ks[:, 1].rearrange("p a b -> p (a b)").bitcast(F32)[:, 0:4 * S].rearrange("p (a j n) -> p a j n", a=2, j=2)
        Q5 = oN[0:DL + 1].rearrange("p (a j) n -> p a j n", a=2)
        K5 = rest[0:DL + 1]
        parts_flat = parts[:].rearrange("p a b c -> p (a b c)")
        qb5 = parts_flat[0:DL, 0:4 * S].rearrange("p (a j n) -> p a j n", a=2, j=2)
        kb5 = Qs[0:DL, 1, 0:4, :].rearrange("p (a j) n -> p a j n", a=2)

        wq, wk, wv = (Wqkv[:, i * C * D:(i + 1) * C * D].rearrange("p (c n) -> p c n", c=C) for i in range(3))
        wo = Wo[:, 0:G * D].rearrange("p (g n) -> p g n", g=G)

        def v_(name, i=0):
            return vec[:, VCOL[name] + i:VCOL[name] + i + 1]

        def spread(cols, n):
            return bass.AP(tensor=cols.tensor, offset=cols.offset, ap=[list(cols.ap[0]), [0, n]])

        psS = [ps(f"psS{i}", [P, S]) for i in range(2)]
        psT = [ps(f"psT{i}", [P, S]) for i in range(3)]
        psO = ps("psO", [P, S])
        small = [ps(f"small{i}", [P, S]) for i in range(2)]

        block = stack.enter_context(nc.Block())

        @block.sync
        def _(sp):
            def tokens(a):
                return a.rearrange("(t p) d -> p t d", p=P)

            def at_row(a, u):
                a = a[u.b]
                return a if isinstance(u.b, int) else bass.AP(tensor=a.tensor, offset=sp.snap(a.offset), ap=a.ap)

            def rows_to_stack(place, who, u, g):
                use = f"m{g}"
                sp.wait_ge(small_read[place.bank(who, use)], place.fills(who, use) + 2)
                sp.dma_start(Qs[ROWS:KROWS, u.parity, 4 * g:4 * g + 4, :], nrows[:, g % 2, :])\
                    .then_inc(sem[f"rows_in{g % 2}"], 16)

            def parts_to_stack(u, i, part):
                dst, slots, done = ((Qs, Q_SLOTS, "q_stacked"), (Ks, K_SLOTS, "k_stacked"))[i]
                ready = ("high", "mid", "low")[part]
                sp.wait_ge(sem[ready], count(ready, u, 2 * i + 2))
                for k, p in enumerate(slots):
                    if p == part:
                        sp.dma_start(dst[DH * k:DH * (k + 1), u.parity, :, :], parts[:, i, part, :]).then_inc(sem[done], 16)

            def store(place, u):
                use = "zb" if u.s in MLP else "y1"
                dst = tokens(at_row(x_mid, u))
                sp.wait_ge(small_read[place.bank("prev", use)], place.fills("prev", use) + 2)
                sp.dma_start(dst, xe[:]).then_inc(sem["x_out"], 16)

            def body(place, prev, cur, nxt):
                if nxt is not None:
                    src = tokens(at_row(x if nxt.s == 0 else x_mid, nxt))
                    if positive(n := count("normed", nxt, 0)):
                        sp.wait_ge(sem["normed"], n)
                    sp.dma_start(xw[:], src).then_inc(sem["x_in"], 16)
                    if nxt.s == 0:
                        src = tokens(at_row(ctx, nxt))
                        if positive(n := count("pens", nxt, 0)):
                            sp.wait_ge(sem["pens"], n)
                        sp.dma_start(cw, src).then_inc(sem["ctx_in"], 16)
                        for i, m in enumerate((maskB, maskBT)):
                            sp.dma_start(masks[:, i, :].rearrange("p (t n) -> p t n", t=T),
                                         at_row(m, nxt).rearrange("(t p) n -> p t n", p=P)).then_inc(sem["mask_in"], 16)
                    elif nxt.s not in OWN_KEYS:
                        sp.dma_start(cT[:], at_row(ctxT, nxt).rearrange("(c p) n -> p c n", p=P)).then_inc(sem["ctx_in"], 16)
                if prev is not None:
                    src = tokens(at_row(x if prev.s == 0 else x_mid, prev))
                    if positive(n := count("x_out", prev, 0)):
                        sp.wait_ge(sem["x_out"], n)
                    sp.dma_start(xe[:], src).then_inc(sem["xe_in"], 16)
                if cur is not None:
                    rows_to_stack(place, "cur", cur, 1)
                if prev is not None and prev.s not in MLP:
                    store(place, prev)
                if nxt is not None:
                    for part in range(3):
                        parts_to_stack(nxt, 0, part)
                    parts_to_stack(nxt, 1, 0)
                if cur is not None:
                    rows_to_stack(place, "cur", cur, 2)
                if nxt is not None:
                    for part in (1, 2):
                        parts_to_stack(nxt, 1, part)
                if cur is not None:
                    rows_to_stack(place, "cur", cur, 3)
                if prev is not None and prev.s in MLP:
                    store(place, prev)
                if nxt is not None:
                    rows_to_stack(place, "nxt", nxt, 0)

            for dst, src in ((vec[:], vecs), (ident[:], eye), (pickf[:], pick),
                             (trif[:, 0], tri), (trif[:, 1], triT)):
                sp.dma_start(dst, src).then_inc(consts_in, 16)
            sp.dma_start(Wqkv[:], wa[0, :, 0:N_QKV]).then_inc(qkv_in, 16)
            sp.dma_start(Wo[:], wa[0, :, N_QKV:]).then_inc(wo_in, 16)
            sp.dma_start(W1[:], wm1[0]).then_inc(wm_in, 16)
            sp.dma_start(W2[:], wm2[0]).then_inc(wm_in, 16)
            for n, _ in enumerate(walk(sp, body)):
                s, kind = divmod(n - 1, 3)
                if n >= 1 and s < 4 and kind == 1:
                    sp.dma_start(Wqkv[:], wa[s + 1, :, 0:N_QKV]).then_inc(qkv_in, 16)
                if n >= 1 and s < 5 and kind == 0:
                    if s:
                        sp.wait_ge(sem["x_out"], AHEAD["x_out"] + 16 * B * s)
                        sp.dma_start(Wo[:], wa[s, :, N_QKV:]).then_inc(wo_in, 16)
                    if s in (1, 3):
                        sp.dma_start(W1[:], wm1[(s + 1) // 2]).then_inc(wm_in, 16)
                        sp.dma_start(W2[:], wm2[(s + 1) // 2]).then_inc(wm_in, 16)
                    if s == 1:
                        for i, m in enumerate((maskS, maskST)):
                            sp.dma_start(masks[:, i, :].rearrange("p (t n) -> p t n", t=T),
                                         m.rearrange("(t p) n -> p t n", p=P)).then_inc(maskS_in, 16)

            sp.wait_ge(sem["x_out"], AHEAD["x_out"] + 16 * B * 5)
            for i, dst in enumerate((Wq5[:], Wk5, Wv5, Wo5)):
                sp.dma_start(dst, w5[i].rearrange("p (c n) -> p c n", c=NP if i == 3 else C)).then_inc(w5_in, 16)
            with sp.Fori(0, B) as b:
                u = Unit(5, b, 0)
                sp.wait_ge(sem["x_out"], count("x_out", u, 0))
                sp.dma_start(xw[:], tokens(x_mid[b])).then_inc(sem["x_in"], 16)
                sp.dma_start(cT[:], ctxT[b].rearrange("(c p) n -> p c n", p=P)).then_inc(sem["ctx_in"], 16)
                sp.wait_ge(small_read[last_bank("y1")], last_fills(b, "y1") + 2)
                sp.dma_start(tokens(out[b]), xw[:]).then_inc(sem["x_out"], 16)
            sp.wait_ge(sem["x_out"], AHEAD["x_out"] + 16 * B * len(STAGES))

        @block.tensor
        def _(pe):
            def transposes(dst, c, src):
                for t in range(T):
                    last = nc.tensor.transpose(dst[:, t * P:(t + 1) * P], src[:, t, c * P:(c + 1) * P], ident[:])
                return last

            def projection(dst, w, cols, src):
                for c in range(C):
                    last = nc.tensor.matmul(dst[:], w[:, c, cols], src[:, c, :], start=c == 0, stop=c == C - 1)
                return last

            def token_major(dst, tiles, src, n, w):
                for i, t in enumerate(tiles):
                    for c in range(n):
                        last = nc.tensor.matmul(dst[:, i * D:(i + 1) * D], src[:, c, t * P:(t + 1) * P], w[:, c, :],
                                                start=c == 0, stop=c == n - 1)
                return last

            def max_scores(u, i, j):
                g, qt = divmod(i, T)
                h, q = 4 * g + j, u.parity
                n = (qt + 1) * P if u.s == CAUSAL else S
                if i == 0 and j == 0:
                    pe.wait_ge(sem["q_stacked"], count("q_stacked", u, 96))
                    pe.wait_ge(sem["k_stacked"], count("k_stacked", u, 96))
                    if u.s == 0:
                        pe.wait_ge(sem["pens"], count("pens", u, 1))
                if positive(k := count("s_read", u, 4 * i + j - 1)):
                    pe.wait_ge(sem["s_read"], k)
                dst = psS[j % 2]
                last = nc.tensor.matmul(dst[:, 0:n], Qs[0:ROWS, q, h, qt * P:(qt + 1) * P], Ks[0:ROWS, q, h, 0:n],
                                        start=True, stop=u.s not in (*MASKED, CAUSAL))
                if u.s in MASKED:
                    last = nc.tensor.matmul(dst[:], identb[:], pens[:, 0, qt * S:(qt + 1) * S], start=False, stop=True)
                if u.s == CAUSAL:
                    last = nc.tensor.matmul(dst[:, n - P:n], identb[:], trib[:, 0, :], start=False, stop=True)
                last.then_inc(sem["s_full"], 1)

            def exp_scores(u, i, j):
                g, kt = divmod(i, T)
                h, q, at = 4 * g + j, u.parity, 4 * i + j
                q0 = kt * P if u.s == CAUSAL else 0
                if kt == 0 and j == 0:
                    pe.wait_ge(sem[f"rows_in{g % 2}"], count(f"rows_in{g % 2}", u, 16 * (g // 2 + 1)))
                if u.s == 0 and at == 0:
                    pe.wait_ge(sem["pens"], count("pens", u, 2))
                if at >= 3 or at == 0:
                    if positive(k := count("exp_done", u, at - 2 if at else 0)):
                        pe.wait_ge(sem["exp_done"], k)
                dst = psT[at % 3]
                last = nc.tensor.matmul(dst[:, q0:S], Ks[0:KROWS, q, h, kt * P:(kt + 1) * P], Qs[0:KROWS, q, h, q0:S],
                                        start=True, stop=u.s not in (*MASKED, CAUSAL))
                if u.s in MASKED:
                    last = nc.tensor.matmul(dst[:], identb[:], pens[:, 1, kt * S:(kt + 1) * S], start=False, stop=True)
                if u.s == CAUSAL:
                    last = nc.tensor.matmul(dst[:, q0:q0 + P], identb[:], trib[:, 1, :], start=False, stop=True)
                last.then_inc(sem["st_full"], 1)

            def outputs(u, i):
                g, kt = divmod(i, T)
                q0 = kt * P if u.s == CAUSAL else 0
                pe.wait_ge(sem["exp_done"], count("exp_done", u, 4 * i + 4))
                if kt == 0 and positive(k := count("o_out", u, g)):
                    pe.wait_ge(sem["o_out"], k)
                for j in range(4):
                    last = nc.tensor.matmul(psO[32 * j:32 * j + 32, q0:S], V[:, u.parity, kt, 4 * g + j, :],
                                            probs[:, i % 2, j, q0:S], start=kt == 0, stop=kt == T - 1)
                last.then_inc(sem["pv_done"], 1)

            def fill(place, who, use, prev, cur, nxt):
                u = {"prev": prev, "cur": cur, "nxt": nxt}[who]
                bank = place.bank(who, use)
                dst = small[bank]
                kind, part = use[0], use[1:]
                if kind == "x":
                    pe.wait_ge(sem["normed"], count("normed", u, 1))
                if kind == "c":
                    pe.wait_ge(sem["normed"], count("normed", u, 2))
                if use == "h0":
                    pe.wait_ge(sem["normed_m"], count("normed_m", u, 1))
                if use == "q0":
                    pe.wait_ge(small_read[place.bank("nxt", "x0")], place.fills("nxt", "x0") + 2)
                    pe.wait_ge(small_read[place.bank("nxt", "x1")], place.fills("nxt", "x1") + 2)
                if use == "k0" and u.s == 0:
                    pe.wait_ge(small_read[place.bank("nxt", "c0")], place.fills("nxt", "c0") + 2)
                    pe.wait_ge(small_read[place.bank("nxt", "c1")], place.fills("nxt", "c1") + 2)
                elif use == "k0" and u.s not in OWN_KEYS:
                    pe.wait_ge(sem["ctx_in"], count("ctx_in", u, 16))
                if kind == "m":
                    pe.wait_ge(sem["split"], count("split", u, 4 * (int(part) + 1)))
                if kind == "s":
                    pe.wait_ge(sem["o_out"], count("o_out", u, int(part) + 1))
                if kind == "r":
                    pe.wait_ge(small_read[place.bank(who, "s" + part)], place.fills(who, "s" + part) + 2)
                if use == "q0":
                    pe.wait_ge(qkv_in, 16 * (u.s + 1))
                if use == "y0":
                    pe.wait_ge(wo_in, 16 * (u.s + 1))
                if use == "y0" and u.s == 2:
                    pe.wait_ge(sem["o_valid"], count("o_valid", u, G))
                elif use == "y0":
                    pe.wait_ge(sem["o_scaled"], count("o_scaled", u, G))
                if use == "fa0":
                    pe.wait_ge(small_read[place.bank("prev", "h0")], place.fills("prev", "h0") + 2)
                    pe.wait_ge(small_read[place.bank("prev", "h1")], place.fills("prev", "h1") + 2)
                if kind == "z":
                    for f in (f"f{part}2", f"f{part}3"):
                        pe.wait_ge(small_read[place.bank("prev", f)], place.fills("prev", f) + 2)
                pe.wait_ge(small_read[bank], place.fills(who, use) + 1)
                if kind in "xch":
                    last = transposes(dst, int(part), cn if kind == "c" else xn)
                elif kind in "qkv":
                    keys = hT if u.s in OWN_KEYS else cT
                    i = int(part)
                    if kind == "v":
                        last = token_major(dst, (2 * i, 2 * i + 1), keys, C, wv)
                    else:
                        last = projection(dst, wq if kind == "q" else wk, slice(i * P, (i + 1) * P), hT if kind == "q" else keys)
                elif kind == "m":
                    for qt in range(T):
                        last = nc.tensor.matmul(dst[0:12, qt * P:(qt + 1) * P],
                                                nparts[:, int(part) % 2, qt, :, :].rearrange("p a b -> p (a b)"), identb[:],
                                                start=True, stop=True)
                elif kind == "s":
                    for qt in range(T):
                        last = nc.tensor.matmul(dst[:, 4 * qt:4 * qt + 4], oT[:, int(part) % 2, qt * P:(qt + 1) * P], pickf[:],
                                                start=True, stop=True)
                elif kind == "r":
                    for at in range(4 * T):
                        qt, j = divmod(at, 4)
                        last = nc.tensor.matmul(dst[32 * j:32 * j + 32, qt * P:(qt + 1) * P],
                                                spread(recip[:, int(part) % 2, at:at + 1], 32), ident[:],
                                                start=True, stop=True)
                elif kind == "y":
                    i = int(part)
                    last = token_major(dst, (2 * i, 2 * i + 1), oN, G, wo)
                elif kind == "f":
                    half, pair = "ab".index(part[0]), int(part[1])
                    for k in range(2):
                        m = 2 * pair + k
                        for c in range(C):
                            last = nc.tensor.matmul(dst[:, k * D:(k + 1) * D], W1[:, c, m * P:(m + 1) * P],
                                                    hT[:, c, half * D:(half + 1) * D], start=c == 0, stop=c == C - 1)
                elif kind == "z":
                    last = token_major(dst, (0, 1), gel, FC, W2)
                else:
                    for kt in range(T):
                        last = nc.tensor.matmul(dst[:], onesb[:], pens[:, 1, kt * S:(kt + 1) * S], start=kt == 0, stop=kt == T - 1)
                last.then_inc(small_full[bank], 1)

            def body(place, prev, cur, nxt):
                for i in range(STEPS):
                    for half in range(2):
                        for j in (2 * half, 2 * half + 1):
                            if cur is not None and i + LEAD < STEPS:
                                max_scores(cur, i + LEAD, j)
                            if nxt is not None and i + LEAD >= STEPS:
                                max_scores(nxt, i + LEAD - STEPS, j)
                            if cur is not None:
                                exp_scores(cur, i, j)
                        if half == 0 and i == 0 and prev is not None:
                            outputs(prev, STEPS - 1)
                        if half == 0 and i > 0 and cur is not None:
                            outputs(cur, i - 1)
                        for who, use in place.body.at(2 * i + half):
                            fill(place, who, use, prev, cur, nxt)

            pe.wait_ge(consts_in, 16 * 5)
            pe.wait_ge(consts_set, 3)
            pe.wait_ge(wm_in, 32)
            for n, _ in enumerate(walk(pe, body)):
                s, kind = divmod(n - 1, 3)
                if n >= 1 and s in (1, 3) and kind == 2:
                    pe.wait_ge(wm_in, 32 * ((s + 1) // 2 + 1))
                if n >= 1 and s == 1 and kind == 1:
                    pe.wait_ge(pensS, 1)

            def last_unit(u, b):
                def take(use):
                    return small[last_bank(use)]

                pe.wait_ge(sem["normed"], count("normed", u, 1))
                for c in range(C):
                    use = f"x{c}"
                    pe.wait_ge(small_read[last_bank(use)], last_fills(b, use) + 1)
                    transposes(take(use), c, xn).then_inc(small_full[last_bank(use)], 1)
                pe.wait_ge(sem["ctx_in"], count("ctx_in", u, 16))
                for i in range(2 * T):
                    t, half = divmod(i, 2)
                    use = f"v{i}"
                    pe.wait_ge(small_read[last_bank(use)], last_fills(b, use) + 1)
                    for c in range(C):
                        last = nc.tensor.matmul(take(use)[:], cT[:, c, t * P:(t + 1) * P], Wv5[:, c, half * S:(half + 1) * S],
                                                start=c == 0, stop=c == C - 1)
                    last.then_inc(small_full[last_bank(use)], 1)

                def project(m, letter):
                    use = f"{letter}{m}"
                    pe.wait_ge(small_read[last_bank(use)], last_fills(b, use) + 1)
                    projection(take(use), Wq5 if letter == "q" else Wk5, slice(m * P, (m + 1) * P),
                               hT if letter == "q" else cT).then_inc(small_full[last_bank(use)], 1)

                def max_scores5(m, qt):
                    if qt == 0:
                        pe.wait_ge(sem["low5"], count("low5", u, 2 * m + 2))
                    for j in range(2):
                        at = 8 * m + 2 * qt + j
                        pe.wait_ge(sem["s_read"], count("s_read", u, at - 1))
                        nc.tensor.matmul(psS[j][:], qb5[:, m % 2, j, qt * P:(qt + 1) * P], kb5[:, m % 2, j, :],
                                         start=True, stop=True).then_inc(sem["s_full"], 1)

                def max_rows(m):
                    pe.wait_ge(sem["s_read"], count("s_read", u, 8 * m + 8))
                    for j in range(2):
                        use = f"m{m}" + "ab"[j]
                        pe.wait_ge(small_read[last_bank(use)], last_fills(b, use) + 1)
                        for qt in range(T):
                            last = nc.tensor.matmul(take(use)[DL:DL + 1, qt * P:(qt + 1) * P], nmax[:, m % 2, qt, j:j + 1],
                                                    ident[:], start=True, stop=True)
                        last.then_inc(small_full[last_bank(use)], 1)

                def exp_scores5(m, kt):
                    for j in range(2):
                        at = 8 * m + 2 * kt + j
                        if kt == 0:
                            use = f"{'qk'[j]}{m}"
                            pe.wait_ge(small_read[last_bank(use)], last_fills(b, use) + 2)
                            use = f"m{m}" + "ab"[j]
                            pe.wait_ge(small_read[last_bank(use)], last_fills(b, use) + 2)
                        pe.wait_ge(sem["exp_done"], count("exp_done", u, at - 1))
                        nc.tensor.matmul(psT[j][:], K5[:, m % 2, j, kt * P:(kt + 1) * P], Q5[:, m % 2, j, :],
                                         start=True, stop=True).then_inc(sem["st_full"], 1)

                def outputs5(m, kt):
                    pe.wait_ge(sem["exp_done"], count("exp_done", u, 8 * m + 2 * kt + 2))
                    if kt == 0:
                        pe.wait_ge(sem["o_out"], count("o_out", u, m))
                    for j in range(2):
                        h = 2 * m + j
                        last = nc.tensor.matmul(psO[DL * j:DL * (j + 1), :], V5[:, kt, h * DL:(h + 1) * DL],
                                                probs[:, kt % 2, j, :], start=kt == 0, stop=kt == T - 1)
                    last.then_inc(sem["pv_done"], 1)

                def sums(m):
                    use = f"s{m}"
                    pe.wait_ge(sem["summed"], count("summed", u, 3 * m + 3))
                    pe.wait_ge(small_read[last_bank(use)], last_fills(b, use) + 1)
                    for j in range(2):
                        last = nc.tensor.matmul(take(use)[DL * j:DL * (j + 1), :], onesf[:], pacc[:, m % 2, j, :],
                                                start=True, stop=True)
                    last.then_inc(small_full[last_bank(use)], 1)

                pe.wait_ge(small_read[last_bank("x0")], last_fills(b, "x0") + 2)
                pe.wait_ge(small_read[last_bank("x1")], last_fills(b, "x1") + 2)
                project(0, "q")
                project(0, "k")
                for qt in range(T):
                    max_scores5(0, qt)
                max_rows(0)
                for m in range(NP):
                    for kt in range(T):
                        exp_scores5(m, kt)
                        if m + 1 < NP:
                            if kt < 2:
                                project(m + 1, "qk"[kt])
                            else:
                                max_scores5(m + 1, 2 * kt - 4)
                                max_scores5(m + 1, 2 * kt - 3)
                        if kt == 0 and m:
                            sums(m - 1)
                        outputs5(m, kt)
                    if m + 1 < NP:
                        max_rows(m + 1)
                sums(NP - 1)
                pe.wait_ge(sem["o_scaled"], count("o_scaled", u, NP))
                for i in range(2):
                    use = f"y{i}"
                    pe.wait_ge(small_read[last_bank(use)], last_fills(b, use) + 1)
                    token_major(take(use), (2 * i, 2 * i + 1), o5, NP, Wo5).then_inc(small_full[last_bank(use)], 1)

            pe.wait_ge(w5_in, 16 * 4)
            pe.wait_ge(ones_row, 1)
            with pe.Fori(0, B) as b:
                last_unit(Unit(5, b, 0), b)

        @block.scalar
        def _(act):
            def exponentials(u, i, j):
                at = 4 * i + j
                q0 = (i % T) * P if u.s == CAUSAL else 0
                act.wait_ge(sem["st_full"], count("st_full", u, at + 1))
                if j == 0 and positive(k := count("pv_done", u, i - 1)):
                    act.wait_ge(sem["pv_done"], k)
                nc.scalar.activation(probs[:, i % 2, j, q0:S], psT[at % 3][:, q0:S], ACT.Exp, scale=float(DH) ** -0.5)\
                    .then_inc(sem["exp_done"], 1)

            def take_outputs(u, g):
                act.wait_ge(sem["pv_done"], count("pv_done", u, T * (g + 1)))
                if positive(k := count("o_scaled", u, g - 1)):
                    act.wait_ge(sem["o_scaled"], k)
                nc.scalar.activation(oT[:, g % 2, :], psO[:], ACT.Copy).then_inc(sem["o_out"], 1)

            def take(place, who, use, prev, cur, nxt):
                u = {"prev": prev, "cur": cur, "nxt": nxt}[who]
                kind, part = use[0], use[1:]
                if kind not in "xchqkmf":
                    return
                bank = place.bank(who, use)
                src = small[bank]
                act.wait_ge(small_full[bank], place.fills(who, use) + 1)
                if kind in "xch":
                    c = int(part)
                    gain, bias = {"x": (f"g{u.s}", f"b{u.s}"), "c": ("gc", "bc"), "h": (f"gm{u.s}", f"bm{u.s}")}[kind]
                    nc.scalar.activation((cT if kind == "c" else hT)[:, c, :], src[:], ACT.Identity, bias=v_(bias, c),
                                         scale=v_(gain, c)).then_inc(small_read[bank], 1)
                elif kind in "qk":
                    i, c = "qk".index(kind), int(part)
                    bias = v_(f"{kind}b{u.s}", c) if u.s in BIASED else 0.0
                    nc.scalar.activation(parts[:, i, 0, c * S:(c + 1) * S], src[:], ACT.Identity, bias=bias).then_inc(sem["high"], 1)
                elif kind == "m":
                    nc.scalar.activation(nrows[:, int(part) % 2, :], src[0:12, :], ACT.Copy).then_inc(small_read[bank], 1)
                else:
                    for k in range(2):
                        m = 2 * int(part[1]) + k
                        last = nc.scalar.activation(gel[:, m, :], src[:, k * D:(k + 1) * D], ACT.Gelu, bias=v_(f"f{u.s}", m))
                    last.then_inc(small_read[bank], 1)

            def middle(place, use):
                i, c = "qk".index(use[0]), int(use[1])
                act.wait_ge(small_read[place.bank("nxt", use)], place.fills("nxt", use) + 2)
                nc.scalar.activation(parts[:, i, 1, c * S:(c + 1) * S], rest[:, i, c, :], ACT.Copy).then_inc(sem["mid"], 1)

            def penalties(i):
                return nc.scalar.activation(pens[:, i, :], masks[:, i, :], ACT.Copy, scale=-BIG)

            def body(place, prev, cur, nxt):
                for slot in range(SLOTS + 1):
                    i, half = divmod(slot, 2)
                    if cur is not None and i < STEPS:
                        exponentials(cur, i, 2 * half)
                        exponentials(cur, i, 2 * half + 1)
                    if slot == 1 and prev is not None:
                        take_outputs(prev, G - 1)
                    if half == 1 and i % T == 0 and i and cur is not None:
                        take_outputs(cur, i // T - 1)
                    for who, use in place.body.at(slot - 1):
                        take(place, who, use, prev, cur, nxt)
                    for who, use in place.body.at(slot - 3):
                        if use[0] in "qk":
                            middle(place, use)
                    if nxt is not None and nxt.s == 0 and slot == 2 * (STEPS - LEAD) - 1:
                        act.wait_ge(sem["mask_in"], count("mask_in", nxt, 32))
                        if cur is not None:
                            act.wait_ge(sem["s_full"], count("s_full", cur, 4 * STEPS))
                        penalties(0).then_inc(sem["pens"], 1)
                if nxt is not None and nxt.s == 0:
                    penalties(1).then_inc(sem["pens"], 1)

            act.wait_ge(consts_in, 16 * 5)
            nc.scalar.activation(identb[:], ident[:], ACT.Copy)
            nc.scalar.activation(trib[:], trif[:], ACT.Copy).then_inc(consts_set, 1)
            for n, _ in enumerate(walk(act, body)):
                if n == 4:
                    act.wait_ge(maskS_in, 32)
                    penalties(0)
                    penalties(1).then_inc(pensS, 1)

            def last_unit(u, b):
                for c in range(C):
                    use = f"x{c}"
                    act.wait_ge(small_full[last_bank(use)], last_fills(b, use) + 1)
                    nc.scalar.activation(hT[:, c, :], small[last_bank(use)][:], ACT.Copy, scale=v_("g5", c))\
                        .then_inc(small_read[last_bank(use)], 1)
                for i in range(0, 2 * T, 2):
                    use = f"v{i}"
                    act.wait_ge(small_full[last_bank(use)], last_fills(b, use) + 1)
                    nc.scalar.activation(V5[:, i // 2, 0:S], small[last_bank(use)][:], ACT.Copy)\
                        .then_inc(small_read[last_bank(use)], 1)

                def even_head(m, letter):
                    use = f"{letter}{m}"
                    dst, low = (Q5, qb5) if letter == "q" else (K5, kb5)
                    src = small[last_bank(use)]
                    act.wait_ge(small_full[last_bank(use)], last_fills(b, use) + 1)
                    nc.scalar.activation(dst[0:DL, m % 2, 0, :], src[0:DL, :], ACT.Copy)
                    nc.scalar.activation(low[:, m % 2, 0, :], src[0:DL, :], ACT.Copy)
                    nc.scalar.activation(low[:, m % 2, 1, :], src[DL:P, :], ACT.Copy).then_inc(sem["low5"], 1)

                def max_rows(m):
                    for j in range(2):
                        use = f"m{m}" + "ab"[j]
                        act.wait_ge(small_full[last_bank(use)], last_fills(b, use) + 1)
                        nc.scalar.activation(Q5[DL:DL + 1, m % 2, j, :], small[last_bank(use)][DL:DL + 1, :], ACT.Copy)\
                            .then_inc(small_read[last_bank(use)], 1)

                def take_outputs5(m):
                    act.wait_ge(sem["pv_done"], count("pv_done", u, T * (m + 1)))
                    act.wait_ge(sem["o_scaled"], count("o_scaled", u, m - 1))
                    nc.scalar.activation(oT[:, m % 2, :], psO[:], ACT.Copy).then_inc(sem["o_out"], 1)

                even_head(0, "q")
                even_head(0, "k")
                max_rows(0)
                for m in range(NP):
                    if m:
                        take_outputs5(m - 1)
                    for kt in range(T):
                        for j in range(2):
                            at = 8 * m + 2 * kt + j
                            act.wait_ge(sem["st_full"], count("st_full", u, at + 1))
                            if j == 0:
                                act.wait_ge(sem["pv_done"], count("pv_done", u, 4 * m + kt - 1))
                                act.wait_ge(sem["summed"], count("summed", u, max(3 * m + (kt - 1 if kt < 2 else 1), 0)))
                            nc.scalar.activation(probs[:, kt % 2, j, :], psT[j][:], ACT.Exp).then_inc(sem["exp_done"], 1)
                        if m + 1 < NP and kt < 2:
                            even_head(m + 1, "qk"[kt])
                    if m + 1 < NP:
                        max_rows(m + 1)
                take_outputs5(NP - 1)

            with act.Fori(0, B) as b:
                last_unit(Unit(5, b, 0), b)

        @block.vector
        def _(dve):
            def token_moments(k, src, name):
                for t in range(T):
                    last = nc.vector.bn_stats(stats[:, k, t, :], src[:, t, :])
                return last

            def aggregate(k):
                for t in range(T):
                    last = nc.vector.bn_aggr(mom[:, k, t, :], stats[:, k, t, :])
                return last

            def before_attention(u, src, n):
                token_moments(0, src, n).then_inc(sem["stats"], 1)
                dve.wait_ge(sem["stats"], count("stats", u, n))
                nc.vector.memset(scratch[:, 3:4], 0.0)
                aggregate(0).then_inc(sem["moments"], 1)

            def normalise(k, src, dst, centre=True):
                for t in range(T):
                    r = rstd[:, k, t:t + 1]
                    if centre:
                        last = nc.vector.tensor_scalar(dst[:, t, :], src[:, t, :], mom[:, k, t, 0:1], r, ALU.subtract, ALU.mult)
                    else:
                        last = nc.vector.tensor_scalar(dst[:, t, :], src[:, t, :], r, None, ALU.mult)
                return last

            def maximum(u, i, j):
                g, qt = divmod(i, T)
                n = (qt + 1) * P if u.s == CAUSAL else S
                dve.wait_ge(sem["s_full"], count("s_full", u, 4 * i + j + 1))
                nc.vector.tensor_reduce(nmax[:, g % 2, qt, j:j + 1], psS[j % 2][:, 0:n], AX, ALU.max, negate=True)\
                    .then_inc(sem["s_read"], 1)

            def take(place, who, use, prev, cur, nxt):
                u = {"prev": prev, "cur": cur, "nxt": nxt}[who]
                kind, part = use[0], use[1:]
                if kind not in "qkvsryzw":
                    return
                bank = place.bank(who, use)
                src = small[bank]
                if kind in "qk":
                    i, c = "qk".index(kind), int(part)
                    dve.wait_ge(sem["high"], count("high", u, 2 * i + c + 1))
                    high = parts[:, i, 0, c * S:(c + 1) * S]
                    if u.s in BIASED:
                        nc.vector.scalar_tensor_tensor(rest[:, i, c, :], src[:], v_(f"{kind}b{u.s}", c), high, ALU.add,
                                                       ALU.subtract).then_inc(small_read[bank], 1)
                    else:
                        nc.vector.tensor_tensor(rest[:, i, c, :], src[:], high, ALU.subtract).then_inc(small_read[bank], 1)
                    return
                dve.wait_ge(small_full[bank], place.fills(who, use) + 1)
                if kind == "v":
                    i = int(part)
                    dst = V[:, u.parity, 2 * i:2 * i + 2, :, 0:DH]
                    values = src[:].rearrange("p (t h d) -> p t h d", t=2, h=H)
                    if u.s in BIASED:
                        bias = v_row.rearrange("p (h d) -> p h d", h=H)
                        for t in range(2):
                            last = nc.vector.tensor_tensor(dst[:, t], values[:, t], bias, ALU.add)
                    else:
                        last = nc.vector.tensor_copy(dst, values)
                    last.then_inc(small_read[bank], 1)
                elif kind == "s":
                    nc.vector.reciprocal(recip[:, int(part) % 2, :], src[:, 0:16]).then_inc(small_read[bank], 1)
                elif kind == "r":
                    g = int(part)
                    nc.vector.tensor_tensor(oN[:, g, :], oT[:, g % 2, :], src[:], ALU.mult).then_inc(sem["o_scaled"], 1)
                    nc.vector.memset(scratch[:, 2:3], 0.0).then_inc(small_read[bank], 1)
                elif kind in "yz":
                    i = int(part) if kind == "y" else "ab".index(part)
                    if use == "y0":
                        dve.wait_ge(sem["biased"], count("biased", u, 1))
                    if use == "za":
                        dve.wait_ge(sem["biased"], count("biased", u, 2))
                    xs = xe[:, 2 * i:2 * i + 2, :]
                    nc.vector.tensor_tensor(xs, xs, src[:].rearrange("p (t n) -> p t n", t=2), ALU.add).then_inc(small_read[bank], 1)
                else:
                    nc.vector.tensor_scalar(valid[:], src[:], 1.0 / BIG, float(S), ALU.mult, ALU.add).then_inc(small_read[bank], 1)
                    dve.wait_ge(small_read[bank], place.fills(who, use) + 2)
                    nc.vector.tensor_scalar(vtmp[:], valid[:], 1.0, None, ALU.min).then_inc(valid_set, 1)
                    dve.wait_ge(valid_set, 1)
                    nc.vector.reciprocal(valid[:], vtmp[:]).then_inc(valid_set, 1)
                    dve.wait_ge(valid_set, 2)
                    nc.vector.tensor_tensor(valid[:], valid[:], vtmp[:], ALU.mult).then_inc(valid_set, 1)

            def body(place, prev, cur, nxt):
                for slot in range(SLOTS + 1):
                    i, half = divmod(slot, 2)
                    for j in (2 * half, 2 * half + 1):
                        if cur is not None and i + LEAD < STEPS:
                            maximum(cur, i + LEAD, j)
                        if nxt is not None and STEPS <= i + LEAD < STEPS + LEAD:
                            maximum(nxt, i + LEAD - STEPS, j)
                    for who, use in place.body.at(slot - 1):
                        take(place, who, use, prev, cur, nxt)
                    if nxt is not None:
                        if slot == 2:
                            dve.wait_ge(sem["x_in"], count("x_in", nxt, 16))
                            before_attention(nxt, xw, 1)
                        if slot == 4:
                            dve.wait_ge(sem["rstd"], count("rstd", nxt, 1))
                            normalise(0, xw, xn).then_inc(sem["normed"], 1)
                        if slot == 5 and nxt.s == 0:
                            dve.wait_ge(sem["ctx_in"], count("ctx_in", nxt, 16))
                            before_attention(nxt, cw, 2)
                        if slot == 7 and nxt.s == 0:
                            dve.wait_ge(sem["rstd"], count("rstd", nxt, 2))
                            normalise(0, cw, cn).then_inc(sem["normed"], 1)
                    if prev is not None and prev.s in MLP:
                        if slot == 9:
                            for use in ("y0", "y1"):
                                dve.wait_ge(small_read[place.bank("prev", use)], place.fills("prev", use) + 2)
                            token_moments(1, xe, 1).then_inc(sem["stats_m"], 1)
                            dve.wait_ge(sem["stats_m"], count("stats_m", prev, 1))
                            nc.vector.memset(scratch[:, 3:4], 0.0)
                            aggregate(1).then_inc(sem["moments_m"], 1)
                        if slot == 11:
                            dve.wait_ge(sem["rstd_m"], count("rstd_m", prev, 1))
                            normalise(1, xe, xn).then_inc(sem["normed_m"], 1)

            nc.vector.memset(V[:], 1.0)
            nc.vector.memset(onesf[:], 1.0)
            nc.vector.memset(onesb[:], 1.0)
            nc.vector.memset(Ks[ROWS:KROWS, :, :, :], 1.0).then_inc(consts_set, 1)
            nc.vector.memset(scratch[:, 2:3], 0.0).then_inc(sem["x_out"], AHEAD["x_out"])
            nc.vector.memset(scratch[:, 3:4], 0.0).then_inc(sem["summed"], AHEAD["summed"])
            nc.vector.memset(scratch[:, 0:1], 0.0).then_inc(small_read[0], 1)
            nc.vector.memset(scratch[:, 1:2], 0.0).then_inc(small_read[1], 1)
            dve.wait_ge(consts_in, 16 * 5)
            for _ in walk(dve, body):
                pass

            def last_unit(u, b):
                dve.wait_ge(sem["x_in"], count("x_in", u, 16))
                before_attention(u, xw, 1)
                dve.wait_ge(sem["rstd"], count("rstd", u, 1))
                normalise(0, xw, xn, centre=False).then_inc(sem["normed"], 1)
                for i in range(1, 2 * T, 2):
                    use = f"v{i}"
                    dve.wait_ge(small_full[last_bank(use)], last_fills(b, use) + 1)
                    nc.vector.tensor_copy(V5[:, i // 2, S:2 * S], small[last_bank(use)][:]).then_inc(small_read[last_bank(use)], 1)

                def odd_head(m, letter):
                    use = f"{letter}{m}"
                    dve.wait_ge(sem["low5"], count("low5", u, 2 * m + (1 if letter == "q" else 2)))
                    dst = Q5 if letter == "q" else K5
                    nc.vector.tensor_copy(dst[0:DL, m % 2, 1, :], small[last_bank(use)][DL:P, :]).then_inc(small_read[last_bank(use)], 1)

                def maxima(m, qt):
                    for j in range(2):
                        dve.wait_ge(sem["s_full"], count("s_full", u, 8 * m + 2 * qt + j + 1))
                        nc.vector.tensor_reduce(nmax[:, m % 2, qt, j:j + 1], psS[j][:], AX, ALU.max, negate=True)\
                            .then_inc(sem["s_read"], 1)

                def scale(m):
                    use = f"s{m}"
                    dve.wait_ge(sem["o_scaled"], count("o_scaled", u, m))
                    dve.wait_ge(small_full[last_bank(use)], last_fills(b, use) + 1)
                    nc.vector.reciprocal(vtmp[:], small[last_bank(use)][:]).then_inc(small_read[last_bank(use)], 1)
                    dve.wait_ge(small_read[last_bank(use)], last_fills(b, use) + 2)
                    dve.wait_ge(sem["o_out"], count("o_out", u, m + 1))
                    nc.vector.tensor_tensor(o5[:, m, :], oT[:, m % 2, :], vtmp[:], ALU.mult).then_inc(sem["o_scaled"], 1)

                odd_head(0, "q")
                odd_head(0, "k")
                for qt in range(T):
                    maxima(0, qt)
                for m in range(NP):
                    for kt in range(T):
                        if m + 1 < NP:
                            if kt < 2:
                                odd_head(m + 1, "qk"[kt])
                            else:
                                maxima(m + 1, 2 * kt - 4)
                                maxima(m + 1, 2 * kt - 3)
                        if kt == 1 and m:
                            scale(m - 1)
                scale(NP - 1)
                for i in range(2):
                    use = f"y{i}"
                    dve.wait_ge(small_full[last_bank(use)], last_fills(b, use) + 1)
                    xs = xw[:, 2 * i:2 * i + 2, :]
                    nc.vector.tensor_tensor(xs, xs, small[last_bank(use)][:].rearrange("p (t n) -> p t n", t=2), ALU.add)\
                        .then_inc(small_read[last_bank(use)], 1)

            dve.wait_ge(sem["x_out"], AHEAD["x_out"] + 16 * B * 5)
            nc.vector.memset(K5[DL:DL + 1, :, :, :], 1.0).then_inc(ones_row, 1)
            with dve.Fori(0, B) as b:
                last_unit(Unit(5, b, 0), b)

        @block.gpsimd
        def _(pool):
            def rsqrt(u, n):
                pool.wait_ge(sem["moments"], count("moments", u, n))
                v = mom[:, 0, :, 1]
                if u.s == 5:
                    nc.gpsimd.tensor_tensor(var[:, 1, :], mom[:, 0, :, 0], mom[:, 0, :, 0], ALU.mult).then_inc(sem["variance"], 1)
                    pool.wait_ge(sem["variance"], count("variance", u, 1))
                    nc.gpsimd.tensor_tensor(var[:, 2, :], mom[:, 0, :, 1], var[:, 1, :], ALU.add).then_inc(sem["variance"], 1)
                    pool.wait_ge(sem["variance"], count("variance", u, 2))
                    v = var[:, 2, :]
                nc.gpsimd.tensor_tensor(var[:, 0, :], v, eps[:, int(u.s == 5), :], ALU.add).then_inc(sem["variance"], 1)
                pool.wait_ge(sem["variance"], count("variance", u, 3 if u.s == 5 else n))
                nc.gpsimd.tensor_tensor(rstd[:, 0, :], var[:, 0, :], mhalf[:], ALU.pow).then_inc(sem["rstd"], 1)

            def rsqrt_mlp(u):
                pool.wait_ge(sem["moments_m"], count("moments_m", u, 1))
                nc.gpsimd.tensor_tensor(var[:, 3, :], mom[:, 1, :, 1], eps[:, 0, :], ALU.add).then_inc(sem["variance_m"], 1)
                pool.wait_ge(sem["variance_m"], count("variance_m", u, 1))
                nc.gpsimd.tensor_tensor(rstd[:, 1, :], var[:, 3, :], mhalf[:], ALU.pow).then_inc(sem["rstd_m"], 1)

            def bias_x(r):
                for t in range(T):
                    last = nc.gpsimd.tensor_tensor(xe[:, t, :], xe[:, t, :], r, ALU.add)
                return last

            def low(u, i, c):
                pool.wait_ge(sem["mid"], count("mid", u, 2 * i + c + 1))
                nc.gpsimd.tensor_tensor(parts[:, i, 2, c * S:(c + 1) * S], rest[:, i, c, :], parts[:, i, 1, c * S:(c + 1) * S],
                                        ALU.subtract).then_inc(sem["low"], 1)

            def split(u, g):
                k = g % 2
                z = zero[:].rearrange("p (t j) -> p t j", t=T)
                pool.wait_ge(sem["s_read"], count("s_read", u, 16 * (g + 1)))
                nc.gpsimd.tensor_tensor(nparts[:, k, :, 0, :], nmax[:, k], z, ALU.add).then_inc(sem["split"], 1)
                pool.wait_ge(sem["split"], count("split", u, 4 * g + 1))
                nc.gpsimd.tensor_tensor(nrest[:, k], nmax[:, k], nparts[:, k, :, 0, :], ALU.subtract).then_inc(sem["split"], 1)
                pool.wait_ge(sem["split"], count("split", u, 4 * g + 2))
                nc.gpsimd.tensor_tensor(nparts[:, k, :, 1, :], nrest[:, k], z, ALU.add).then_inc(sem["split"], 1)
                pool.wait_ge(sem["split"], count("split", u, 4 * g + 3))
                nc.gpsimd.tensor_tensor(nparts[:, k, :, 2, :], nrest[:, k], nparts[:, k, :, 1, :], ALU.subtract).then_inc(sem["split"], 1)

            def invalidate(u, g):
                if u.s == 2:
                    pool.wait_ge(sem["o_scaled"], count("o_scaled", u, g + 1))
                    nc.gpsimd.tensor_tensor(oN[:, g, :], oN[:, g, :], valid[:], ALU.mult).then_inc(sem["o_valid"], 1)

            def body(place, prev, cur, nxt):
                if nxt is not None:
                    rsqrt(nxt, 1)
                if cur is not None:
                    split(cur, 1)
                if prev is not None:
                    pool.wait_ge(sem["xe_in"], count("xe_in", prev, 16))
                    pool.wait_ge(wo_in, 16 * (prev.s + 1))
                    bias_x(o_row).then_inc(sem["biased"], 1)
                    invalidate(prev, 3)
                if nxt is not None:
                    if nxt.s == 0:
                        rsqrt(nxt, 2)
                    low(nxt, 0, 0)
                if prev is not None and prev.s in MLP:
                    rsqrt_mlp(prev)
                    pool.wait_ge(sem["normed_m"], count("normed_m", prev, 1))
                    bias_x(z_row).then_inc(sem["biased"], 1)
                if cur is not None:
                    split(cur, 2)
                if nxt is not None:
                    low(nxt, 0, 1)
                    low(nxt, 1, 0)
                if cur is not None:
                    invalidate(cur, 0)
                if nxt is not None:
                    low(nxt, 1, 1)
                if cur is not None:
                    split(cur, 3)
                    invalidate(cur, 1)
                if nxt is not None:
                    split(nxt, 0)
                if cur is not None:
                    invalidate(cur, 2)

            def last_unit(u):
                rsqrt(u, 1)
                for m in range(NP):
                    for kt in range(1, T):
                        pool.wait_ge(sem["exp_done"], count("exp_done", u, 8 * m + 2 * kt + 2))
                        pool.wait_ge(sem["summed"], count("summed", u, 3 * m + kt - 1))
                        before = probs[:, 0, 0:2, :] if kt == 1 else pacc[:, m % 2]
                        nc.gpsimd.tensor_tensor(pacc[:, m % 2], before, probs[:, kt % 2, 0:2, :], ALU.add).then_inc(sem["summed"], 1)

            nc.gpsimd.memset(eps[:, 0, :], LN_EPS)
            nc.gpsimd.memset(eps[:, 1, :], RMS_EPS)
            nc.gpsimd.memset(mhalf[:], -0.5)
            nc.gpsimd.memset(zero[:], 0.0).then_inc(consts_set, 1)
            pool.wait_ge(consts_set, 3)
            pool.wait_ge(consts_in, 16 * 5)
            for n, _ in enumerate(walk(pool, body)):
                if n == 6:
                    pool.wait_ge(valid_set, 3)
            with pool.Fori(0, B) as b:
                last_unit(Unit(5, b, 0))


def in_chunks(w):
    k, n = w.shape
    return w.reshape(k // P, P, n).transpose(1, 0, 2).reshape(P, -1)


def columns(v):
    return v.reshape(-1, P).T


def by_dim(w):
    n = w.ndim
    return w.reshape(*w.shape[:-1], GB, C, DH).transpose(*range(n - 1), n, n + 1, n - 1).reshape(w.shape)


def strips(w):
    o = np.zeros((G, 4, 32, w.shape[1]), w.dtype)
    o[:, :, :DH] = w.reshape(G, 4, DH, -1)
    return o.reshape(G, P, -1).transpose(1, 0, 2).reshape(P, -1)


def kernel(**inputs):
    import concourse.bacc as bacc
    from concourse.bass_utils import run_bass_kernel_spmd

    a = {k: np.asarray(v) for k, v in inputs.items()}
    L0, L1, L2, L3 = ({k[9:]: v for k, v in a.items() if k.startswith(f"L{i}_xattn_")} for i in range(4))
    qkv = L2["w_qkv"].T
    kv2 = L2["w_kv"].T
    att = [
        (L0["q_w"], L0["kv_w"][:, :D], L0["kv_w"][:, D:], L0["proj_w"]),
        (L1["ca_qw"], L1["ca_kw"], L1["ca_vw"], L1["ca_ow"]),
        (L1["sa_qw"], L1["sa_kw"], L1["sa_vw"], L1["sa_ow"]),
        (qkv[:, :D], qkv[:, D:2 * D], qkv[:, 2 * D:], L2["w_prj1"].T),
        (L2["w_q"].T, kv2[:, :D], kv2[:, D:], L2["w_prj2"].T),
    ]
    none = np.zeros_like(L0["proj_b"])
    biases = [(none, L0["proj_b"], L0["fc2_b"]), (L1["ca_vb"], L1["ca_ob"], none), (L1["sa_vb"], L1["sa_ob"], L1["b2"]),
              (none, L2["b_prj1"], none), (none, L2["b_prj2"], L2["b_fc2"])]
    wa = np.stack([np.concatenate([in_chunks(by_dim(q)), in_chunks(by_dim(k)), in_chunks(v), np.broadcast_to(bv, (P, D)),
                                   strips(o), np.broadcast_to(bo, (P, D)), np.broadcast_to(bz, (P, D))], axis=1)
                   for (q, k, v, o), (bv, bo, bz) in zip(att, biases)])
    mlps = [(L0["fc1_w"], L0["fc2_w"]), (L1["w1"], L1["w2"]), (L2["w_fc1"].T, L2["w_fc2"].T)]
    vectors = {
        "g0": L0["qn_w"], "b0": L0["qn_b"], "gc": L0["cn_w"], "bc": L0["cn_b"],
        "g1": L1["ln1_g"], "b1": L1["ln1_b"], "g2": L1["ln2_g"], "b2": L1["ln2_b"],
        "g3": L2["ln1_g"], "b3": L2["ln1_b"], "g4": L2["ln2_g"], "b4": L2["ln2_b"],
        "g5": L3["norm_w"], "b5": L3["norm_w"],
        "qb1": by_dim(L1["ca_qb"]), "kb1": by_dim(L1["ca_kb"]), "qb2": by_dim(L1["sa_qb"]), "kb2": by_dim(L1["sa_kb"]),
        "gm0": L0["n2_w"], "bm0": L0["n2_b"], "f0": L0["fc1_b"],
        "gm2": L1["ln3_g"], "bm2": L1["ln3_b"], "f2": L1["b1"],
        "gm4": L2["ln3_g"], "bm4": L2["ln3_b"], "f4": L2["b_fc1"],
    }
    pick = np.zeros((P, 4), np.float32)
    pick[DH::32] = np.eye(4)
    upper = np.triu(np.full((P, P), -BIG, np.float32), 1)
    maskB, maskS = a["mask_BxSxS2_bk0"], a["mask_SxS_bk1"]
    arrays = {
        "x": a["x"], "ctx": a["ctx_1024"], "ctxT": a["ctx_1024"].transpose(0, 2, 1),
        "maskB": maskB, "maskBT": maskB.transpose(0, 2, 1), "maskS": maskS, "maskST": maskS.T,
        "vecs": np.concatenate([columns(vectors[n]) for n in VECS], axis=1),
        "wa": wa,
        "wm1": np.stack([in_chunks(w).reshape(P, C, FF) for w, _ in mlps]),
        "wm2": np.stack([in_chunks(w).reshape(P, FC, D) for _, w in mlps]),
        "w5": np.stack([in_chunks(L3[n]) for n in ("wq", "wk", "wv", "wo")]),
        "eye": np.eye(P, dtype=np.float32), "pick": pick, "tri": upper, "triT": upper.T,
    }
    arrays = {k: np.ascontiguousarray(v) for k, v in arrays.items()}
    nc = bacc.Bacc("TRN2", target_bir_lowering=False, num_devices=1)
    args = [nc.dram_tensor(k, v.shape, mybir.dt.from_np(v.dtype), kind="ExternalInput").ap() for k, v in arrays.items()]
    out = nc.dram_tensor("out", (B, S, D), F32, kind="ExternalOutput").ap()
    build(nc, *args, out)
    r = run_bass_kernel_spmd(nc, [arrays], core_ids=[0])
    return r.results[0]["out"]
```
